# Optimizing a Trainium2 kernel written in Bass

```python
import numpy as np
import jax
import jax.numpy as jnp

def _softmax(x, axis=-1):
    return jax.nn.softmax(x, axis=axis)

def _gelu(x):
    return jax.nn.gelu(x, approximate=True)

def _silu(x):
    return jax.nn.silu(x)

def _sigmoid(x):
    return jax.nn.sigmoid(x)

def _layernorm(x, axis=-1, eps=1e-05):
    m = jnp.mean(x, axis=axis, keepdims=True)
    v = jnp.var(x, axis=axis, keepdims=True)
    return (x - m) / jnp.sqrt(v + eps)

def _scatter_add(tgt, idx, src, axis=0):
    return tgt.at[idx].add(src)

def _segment_sum(src, seg, n):
    return jax.ops.segment_sum(src, seg, n)
kernel_name = 'mk_macaron_d1_jaxref_r8_5de910'

def setup_inputs(seed: int=0):
    np.random.seed(seed)
    _w = jnp.asarray

    def _L0_attn_setup():
        import jax, jax.numpy as jnp
        import numpy as np
        BATCH, SEQ, D_MODEL, STATE_DIM = (8, 256, 128, 128)

        def _cayley_circulant_eigenvalues(a_params, n):
            half_n = n // 2
            a_full = jnp.zeros((n,), dtype=a_params.dtype)
            a_full = a_full.at[1:half_n].set(a_params[:half_n - 1])
            a_full = a_full.at[half_n + 1:].set(-a_params[:half_n - 1][::-1])
            omega = jnp.fft.fft(a_full).imag
            w2 = omega * omega
            denom = 1.0 + w2
            return ((1.0 - w2) / denom + 1j * (-2.0 * omega / denom)).astype(jnp.complex64)
        key = jax.random.key(seed)
        k1, k2, k3, k4 = jax.random.split(key, 4)
        u = jax.random.normal(k1, (BATCH, SEQ, D_MODEL), dtype=jnp.float32)
        a_params = jax.random.normal(k2, (STATE_DIM // 2,), dtype=jnp.float32) * 0.1
        B_w = jax.random.normal(k3, (STATE_DIM, D_MODEL), dtype=jnp.float32) / np.sqrt(D_MODEL).astype(np.float32)
        C_w = jax.random.normal(k4, (D_MODEL, STATE_DIM), dtype=jnp.float32) / np.sqrt(STATE_DIM).astype(np.float32)
        D = jnp.zeros((D_MODEL,), dtype=jnp.float32)
        return {'u': u, 'a_params': a_params, 'B_w': B_w, 'C_w': C_w, 'D': D}
    _L0_attn_in = _L0_attn_setup()

    def _L0_ffn_setup():
        import jax, jax.numpy as jnp
        import numpy as np
        B, S, D = (4, 256, 128)
        E = 8
        F = 512
        T = B * S
        CAP = 160
        key = jax.random.key(seed)
        k1, k2, k3, k4 = jax.random.split(key, 4)
        inputs = jax.random.normal(k1, (B, S, D), dtype=jnp.float32)
        gate_w = jax.random.normal(k2, (D, E), dtype=jnp.float32) / np.sqrt(D)
        w1 = jax.random.normal(k3, (E, D, F), dtype=jnp.float32) / np.sqrt(D)
        w2 = jax.random.normal(k4, (E, F, D), dtype=jnp.float32) / np.sqrt(F)
        return {'inputs': inputs, 'gate_w': gate_w, 'w1': w1, 'w2': w2}
    _L0_ffn_in = _L0_ffn_setup()
    _d = {'L0_attn_u': _L0_attn_in['u'], 'L0_attn_a_params': _L0_attn_in['a_params'], 'L0_attn_B_w': _L0_attn_in['B_w'], 'L0_attn_C_w': _L0_attn_in['C_w'], 'L0_attn_D': _L0_attn_in['D'], 'L0_ffn_gate_w': _L0_ffn_in['gate_w'], 'L0_ffn_w1': _L0_ffn_in['w1'], 'L0_ffn_w2': _L0_ffn_in['w2']}
    _x0 = _d['L0_attn_u']
    _d['L0_attn_u'] = jax.random.normal(jax.random.fold_in(jax.random.key(seed), 1), (8, 512, 128), dtype=_x0.dtype)
    del _x0
    return _d

def reference(L0_attn_u, L0_attn_a_params, L0_attn_B_w, L0_attn_C_w, L0_attn_D, L0_ffn_gate_w, L0_ffn_w1, L0_ffn_w2):

    def _L0_attn_ref(u, a_params, B_w, C_w, D):
        import jax, jax.numpy as jnp
        import numpy as np
        BATCH, SEQ, D_MODEL, STATE_DIM = (8, 256, 128, 128)

        def _cayley_circulant_eigenvalues(a_params, n):
            half_n = n // 2
            a_full = jnp.zeros((n,), dtype=a_params.dtype)
            a_full = a_full.at[1:half_n].set(a_params[:half_n - 1])
            a_full = a_full.at[half_n + 1:].set(-a_params[:half_n - 1][::-1])
            omega = jnp.fft.fft(a_full).imag
            w2 = omega * omega
            denom = 1.0 + w2
            return ((1.0 - w2) / denom + 1j * (-2.0 * omega / denom)).astype(jnp.complex64)
        n = B_w.shape[0]
        lambdas = _cayley_circulant_eigenvalues(a_params, n)
        Bu = jnp.einsum('bsd,nd->bsn', u, B_w)

        def step(h, bu_t):
            Wh = jnp.fft.ifft(lambdas * jnp.fft.fft(h.astype(jnp.float32))).real.astype(h.dtype)
            h_new = Wh + bu_t
            return (h_new, h_new)
        h0 = jnp.zeros((u.shape[0], n), dtype=u.dtype)
        _, hs = jax.lax.scan(step, h0, jnp.swapaxes(Bu, 0, 1))
        y = jnp.einsum('sbn,dn->bsd', hs, C_w) + D * u
        return y

    def _L0_ffn_ref(inputs, gate_w, w1, w2):
        import jax, jax.numpy as jnp
        import numpy as np
        B, S, D = (4, 256, 128)
        E = 8
        F = 512
        T = B * S
        CAP = 160
        tokens = inputs.reshape(-1, D)
        logits = tokens @ gate_w
        probs = jax.nn.softmax(logits, axis=-1)
        expert_idx = jnp.argmax(probs, axis=-1)
        mask1 = jax.nn.one_hot(expert_idx, E, dtype=tokens.dtype)
        pos = (jnp.cumsum(mask1, axis=0) - 1.0).astype(jnp.int32)
        sec_mask = mask1[:, :, None] * jax.nn.one_hot(pos, CAP, dtype=tokens.dtype)
        combine_weights = probs[:, :, None] * sec_mask
        expert_input = jnp.einsum('tec,td->ecd', sec_mask, tokens)
        h = jax.nn.relu(jnp.einsum('ecd,edf->ecf', expert_input, w1))
        expert_output = jnp.einsum('ecf,efd->ecd', h, w2)
        out = jnp.einsum('tec,ecd->td', combine_weights, expert_output)
        return out.reshape(inputs.shape)
    x = L0_attn_u
    x = x + 0.5 * _L0_ffn_ref(_layernorm(x, axis=-1), L0_ffn_gate_w, L0_ffn_w1, L0_ffn_w2)
    x = x + _L0_attn_ref(_layernorm(x, axis=-1), L0_attn_a_params, L0_attn_B_w, L0_attn_C_w, L0_attn_D)
    x = x + 0.5 * _L0_ffn_ref(_layernorm(x, axis=-1), L0_ffn_gate_w, L0_ffn_w1, L0_ffn_w2)
    return x

_drawn_inputs = setup_inputs


def setup_inputs(seed=0):
    import zlib

    import numpy as np

    out = dict(_drawn_inputs(seed))
    spreads = {'L0_attn_D': (0.0, 0.8)}
    factors = {}
    for name, (base, spread) in spreads.items():
        noise = np.random.default_rng([zlib.crc32(name.encode()), seed]).standard_normal(out[name].shape)
        drawn = base * np.exp(spread * noise) if base else spread * noise
        out[name] = jnp.asarray(drawn.astype(out[name].dtype))
    for name, factor in factors.items():
        out[name] = (out[name] * factor).astype(out[name].dtype)
    return out
```

```python
import concourse.bass as bass
from concourse import mybir
from contextlib import ExitStack


def macaron_moe_ssm_kernel(nc, x_in, a_params, b_w, c_w, d_skip, gate_w, w1, w2, const_early, const_late, out):
    F32, BF16, I32, U32 = mybir.dt.float32, mybir.dt.bfloat16, mybir.dt.int32, mybir.dt.uint32
    ALU, ACT, AX = mybir.AluOpType, mybir.ActivationFunctionType, mybir.AxisListType.X

    NB, SEQ, D = x_in.shape
    E, _, F = w1.shape
    P = 128
    T = NB * SEQ
    TB = SEQ // P
    NT = T // P
    CAP = 160
    SLOTS = E * CAP
    NS = SLOTS // P
    FC = F // P
    HC = FC // 2
    SKIP = 2.0 * T
    EPS = 1e-5

    ctx = ExitStack()
    with ctx:
        def sb(name, shape, dt=F32):
            return ctx.enter_context(nc.sbuf_tensor(name, shape, dt))

        def sem(name):
            return ctx.enter_context(nc.semaphore(name))

        bank = [ctx.enter_context(nc.psum_tensor(f"bank{i}", [P, 512], F32)) for i in range(8)]

        ce = sb("ce", [P, const_early.shape[1]])
        cl = sb("cl", [P, const_late.shape[1]])
        at = [0]

        def part(n):
            at[0] += n
            return ce[:, at[0] - n:at[0]]

        ident, center, sines = part(P), part(P), part(P)
        iota_part, tri_less_one = part(P), part(P)
        rev, iota_ns, tile_no, place1 = part(E), part(NS), part(NT), part(1)
        basis_in, basis_out, basis_turned = cl[:, 0:2 * P], cl[:, 2 * P:3 * P], cl[:, 3 * P:4 * P]
        iota_bf = sb("iota_bf", [P, P], BF16)
        tri_bf = sb("tri_bf", [P, P], BF16)
        ones_bf = sb("ones_bf", [P, P], BF16)
        restart = sb("restart", [P, E, NT], BF16)
        eps = sb("eps", [P, 1])
        par = sb("par", [P // 2, 1])
        bw = sb("bw", [P, D])
        cw = sb("cw", [P, P])
        dsk = sb("dsk", [P, D])
        gate = sb("gate", [P, E])
        gate_c = sb("gate_c", [P, E])
        w1s = sb("w1s", [P, E, F])
        w2s = sb("w2s", [P, E, FC, D])
        x = sb("x", [P, NT, D])
        x2 = sb("x2", [P, NT, D])
        xT = sb("xT", [P, 2, SEQ])
        top = sb("top", [P, NT])
        is_top = sb("is_top", [P, NT, E])
        key = sb("key", [P, NT, E])
        top_key = sb("top_key", [P, NT])
        chosen = sb("chosen", [P, E, NT], BF16)
        counted = sb("counted", [P, E, NT], BF16)
        own_count = sb("own_count", [P, E, NT])
        count = sb("count", [P, NT])
        over = sb("over", [P, NT])
        slot_f = sb("slot_f", [P, NT])
        slot_i = sb("slot_i", [P, NT], I32)
        split_i = sb("split_i", [P, 2, NT], I32)
        split_f = sb("split_f", [P, 2, NT])
        hot_place = sb("hot_place", [P, NT, P], BF16)
        hot_tile = sb("hot_tile", [P, NT, NS], BF16)
        hot_tok = sb("hot_tok", [P, NT, 2, NS], BF16)
        found = sb("found", [P, 2, NS])
        unfilled = sb("unfilled", [P, NS])
        tok_f = sb("tok_f", [P, NS])
        tok = sb("tok", [P, NS], U32)
        xg = sb("xg", [P, NS, D])
        xc = sb("xc", [P, NS, D])
        xcT = sb("xcT", [P, SLOTS])
        gstat = sb("gstat", [P, NS, 6])
        gmv = sb("gmv", [P, NS, 2])
        gsd = sb("gsd", [P, NS])
        grs = sb("grs", [P, NS])
        lg = sb("lg", [P, NS, E])
        lgx = sb("lgx", [P, NS])
        pe_ = sb("prob_e", [P, NS, E])
        psm = sb("prob_sum", [P, NS])
        prc = sb("prob_rc", [P, NS])
        gscale = sb("gscale", [P, NS])
        hT = sb("hT", [P, 2, FC, CAP])
        eoT = sb("eoT", [P, SLOTS])
        xnew = sb("xnew", [P, NS, D])
        om = sb("om", [P, 4])
        ct = sb("ct", [P, SEQ + 1])
        st = sb("st", [P, SEQ + 1])
        tmp = sb("tmp", [P, 2, SEQ // 2])
        bt = sb("bt", [P, 2 * P])
        cwT = sb("cwT", [P, D])
        g1 = sb("g1", [P, D])
        g2 = sb("g2", [P, D])
        sstat = sb("sstat", [P, TB, 6])
        smv = sb("smv", [P, TB, 2])
        ssd = sb("ssd", [P, TB])
        srs = sb("srs", [P, 2, TB])
        snb = sb("snb", [P, 2, TB])
        u = sb("u", [P, 2, TB, D])
        ud = sb("ud", [P, TB, D])
        w = sb("w", [P, 2, TB, D])
        uT = sb("uT", [P, 2, SEQ])
        vq = sb("vq", [P, SEQ])
        va = sb("va", [P, SEQ])
        vb = sb("vb", [P, SEQ])
        z = sb("z", [P, SEQ])
        zc = sb("zc", [P, 2, SEQ])
        zs = sb("zs", [P, 2, SEQ])

        x1_dram = nc.dram_tensor("x1_scratch", [T, D], F32, kind="Internal").ap()
        x_rows = x_in.rearrange("b s d -> (b s) d")
        out_rows = out.rearrange("b s d -> (b s) d")

        def tiles(rows, b):
            return rows[b * SEQ:(b + 1) * SEQ, :].rearrange("(c p) d -> p c d", p=P)

        d_early, d_late, d_gate, d_par, d_bw, d_cw, d_dsk = (sem(f"d_{n}") for n in
                                                             ("early", "late", "gate", "par", "bw", "cw", "dsk"))
        d_w1 = [sem(f"d_w1_{i}") for i in range(2)]
        d_w2 = [sem(f"d_w2_{i}") for i in range(2)]
        d_x = [sem(f"d_x{b}") for b in range(NB)]
        d_x1 = [sem(f"d_x1_{b}") for b in range(NB)]
        d_fill = sem("d_fill")
        d_gather = [sem(f"d_gather{j}") for j in range(NS)]
        d_scatter = sem("d_scatter")
        d_out = sem("d_out")
        pool_set, pool_chain, dve_chain = sem("pool_set"), sem("pool_chain"), sem("dve_chain")
        set_ps, set_sb = sem("set_ps"), sem("set_sb")
        omega_ps, tables = sem("omega_ps"), sem("tables")
        xT_ps, xT_sb, logits = sem("xT_ps"), sem("xT_sb"), sem("logits")
        marked, ranked, hot, placed, indexed = (sem(n) for n in ("marked", "ranked", "hot", "placed", "indexed"))
        centered, slotT_ps, slotT_sb, slot_logits = (sem(n) for n in ("centered", "slotT_ps", "slotT_sb", "slot_logits"))
        gvar, gsd_r, lg_r, pe_r = (sem(n) for n in ("gvar", "gsd_r", "lg_r", "pe_r"))
        h_ps, h_sb, eo_ps, eo_sb, row_ps, row_sb = (sem(n) for n in ("h_ps", "h_sb", "eo_ps", "eo_sb", "row_ps", "row_sb"))
        svar, ssd_r, snb_r, u_r, w_r = (sem(n) for n in ("svar", "ssd_r", "snb_r", "u_r", "w_r"))
        uT_ps, uT_sb, v_ps, vq_sb, va_r, vb_r, z_r = (sem(n) for n in ("uT_ps", "uT_sb", "v_ps", "vq_sb", "va_r", "vb_r", "z_r"))
        zc_r, zs_r, y_ps, x2_r = (sem(n) for n in ("zc_r", "zs_r", "y_ps", "x2_r"))

        def experts_before(j):
            return -(-(j + 1) * P // CAP)

        def tiles_before(e):
            return -(-(e + 1) * CAP // P)

        pe_steps = [("i", 0), ("i", 1), ("i", 2), ("u", 0), ("i", 3), ("i", 4), ("u", 1), ("d", 0), ("i", 5), ("i", 6),
                    ("u", 2), ("d", 1), ("i", 7), ("i", 8), ("u", 3), ("d", 2), ("i", 9), ("u", 4), ("l", 0), ("d", 3)]
        dve_steps = [("i", j) for j in range(7)] + [("d", 0), ("i", 7), ("i", 8), ("d", 1), ("i", 9), ("d", 2), ("l", 0)]
        sent = 0
        for e in range(4, E + 1):
            if e < E:
                if e + 1 < E:
                    pe_steps.append(("u", e + 1))
                pe_steps.append(("d", e))
            while sent < NS and experts_before(sent) <= e:
                pe_steps.append(("o", sent))
                sent += 1
        out_j = 0
        for e in range(3, E):
            dve_steps.append(("d", e))
            while out_j < NS and experts_before(out_j) <= e:
                dve_steps.append(("o", out_j))
                out_j += 1
        dve_steps += [("o", j) for j in range(out_j, NS)]

        block = ctx.enter_context(nc.Block())

        @block.sync
        def _(sp):
            for b in range(NB):
                sp.dma_start(x[:, b * TB:(b + 1) * TB, :], tiles(x_rows, b)).then_inc(d_x[b], 16)
            for i in range(2):
                h = slice(i * E // 2, (i + 1) * E // 2)
                sp.dma_start(w1s[:, h, :], w1[h].rearrange("e d f -> d e f")).then_inc(d_w1[i], 16)
                for e in range(i * E // 2, (i + 1) * E // 2):
                    sp.dma_start(w2s[:, e, :, :], w2[e].rearrange("(c p) d -> p c d", p=P)).then_inc(d_w2[i], 16)
            for b in range(NB):
                sp.wait_ge(d_x[b], 16)
                sp.dma_start(tiles(x1_dram, b), x[:, b * TB:(b + 1) * TB, :]).then_inc(d_fill, 16)
            sp.wait_ge(d_fill, 16 * NB)
            sp.wait_ge(d_scatter, 16 * NS)
            sp.wait_ge(xT_ps, NB)
            for b in range(NB):
                sp.dma_start(x[:, b * TB:(b + 1) * TB, :], tiles(x1_dram, b)).then_inc(d_x1[b], 16)
            for b in range(NB):
                sp.wait_ge(x2_r, b + 1)
                sp.dma_start(tiles(out_rows, b), x2[:, b * TB:(b + 1) * TB, :]).then_inc(d_out, 16)
            sp.wait_ge(d_out, 16 * NB)
            sp.wait_ge(d_scatter, 16 * NS * 2)

        @block.gpsimd
        def _(pool):
            links = [0]

            def link(ins):
                links[0] += 1
                ins.then_inc(pool_chain, 1)
                pool.wait_ge(pool_chain, links[0])

            nc.gpsimd.memset(ones_bf[:, :], 1.0)
            nc.gpsimd.memset(eps[:, :], EPS)
            link(nc.gpsimd.memset(restart[:, :, :], 1.0))
            nc.gpsimd.memset(restart[:, :, 0:1], 0.0)
            pool.wait_ge(d_early, 16)
            nc.gpsimd.tensor_copy(iota_bf[:, :], iota_part)
            nc.gpsimd.tensor_copy(tri_bf[:, :], tri_less_one)
            link(nc.gpsimd.memset(xg[:, :, :], 0.0))
            nc.gpsimd.memset(ud[0:1, 0:1, 0:1], 0.0).then_inc(pool_set, 1)

            def gather(n):
                pool.wait_ge(indexed, n + 1)
                if n == 1:
                    pool.wait_ge(d_out, 16 * NB)
                    pool.wait_ge(row_sb, NS)
                for j in range(NS):
                    pool.indirect_dma_start(xg[:, j, :], None, (x_rows, out_rows)[n],
                                            bass.IndirectOffsetOnAxis(ap=tok[:, j:j + 1], axis=0),
                                            bounds_check=T - 1, oob_is_err=False).then_inc(d_gather[j], 16)

            def scatter(n):
                if n == 0:
                    pool.wait_ge(d_fill, 16 * NB)
                for j in range(NS):
                    pool.wait_ge(row_sb, n * NS + j + 1)
                    pool.indirect_dma_start((x1_dram, out_rows)[n],
                                            bass.IndirectOffsetOnAxis(ap=tok[:, j:j + 1], axis=0),
                                            xnew[:, j, :], None,
                                            bounds_check=T - 1, oob_is_err=False).then_inc(d_scatter, 16)

            gather(0)
            scatter(0)
            pool.wait_ge(d_dsk, 16)
            pool.wait_ge(tables, 1)

            def skip_term(b):
                pool.wait_ge(u_r, b + 1)
                if b >= 1:
                    pool.wait_ge(w_r, b)
                link(nc.gpsimd.tensor_tensor(ud[:, :, :], u[:, b % 2, :, :],
                                             dsk[:, :].unsqueeze(1).broadcast_to([P, TB, D]), ALU.mult))
                if b >= 2:
                    pool.wait_ge(x2_r, b - 1)
                nc.gpsimd.tensor_tensor(w[:, b % 2, :, :], ud[:, :, :], x[:, b * TB:(b + 1) * TB, :],
                                        ALU.add).then_inc(w_r, 1)

            skip_term(0)
            for b in range(NB):
                pool.wait_ge(vq_sb, b + 1)
                if b >= 1:
                    pool.wait_ge(z_r, b)
                nc.gpsimd.tensor_tensor(vb[:, :], vq[:, :], st[:, 0:SEQ], ALU.mult).then_inc(vb_r, 1)
                if b + 1 < NB:
                    skip_term(b + 1)
                pool.wait_ge(z_r, b + 1)
                if b >= 2:
                    pool.wait_ge(y_ps, b - 1)
                nc.gpsimd.tensor_tensor(zs[:, b % 2, :], z[:, :], st[:, 0:SEQ], ALU.mult).then_inc(zs_r, 1)
            gather(1)
            scatter(1)

        @block.scalar
        def _(act):
            act.dma_start(ce[:, :], const_early).then_inc(d_early, 16)
            act.dma_start(gate[:, :], gate_w).then_inc(d_gate, 16)
            act.dma_start(par[:, :], a_params.rearrange("(n o) -> n o", o=1)).then_inc(d_par, 16)
            act.dma_start(bw[:, :], b_w).then_inc(d_bw, 16)
            act.dma_start(cw[:, :], c_w).then_inc(d_cw, 16)
            act.dma_start(dsk[:, :], d_skip.partition_broadcast(P)).then_inc(d_dsk, 16)
            act.dma_start(cl[:, :], const_late).then_inc(d_late, 16)

            def copy_xT(k):
                act.wait_ge(xT_ps, k + 1)
                if k >= 2:
                    act.wait_ge(logits, k - 1)
                src = bank[k % 2 if k < NB else 1]
                nc.scalar.copy(xT[:, k % 2, :], src[:, :]).then_inc(xT_sb, 1)

            def slots(n):
                def slot_in(j):
                    act.wait_ge(slotT_ps, n * NS + j + 1)
                    nc.scalar.copy(xcT[:, j * P:(j + 1) * P],
                                   bank[j % 2][:, 0:P]).then_inc(slotT_sb, 1)

                def relu(e):
                    for half in range(2):
                        act.wait_ge(h_ps, n * 2 * E + 2 * e + half + 1)
                        if e >= 2:
                            act.wait_ge(eo_ps, n * E + e - 1)
                        nc.scalar.activation(hT[:, e % 2, half * HC:(half + 1) * HC, :],
                                             bank[4 + half][:, 0:HC * CAP]
                                             .rearrange("p (c s) -> p c s", c=HC), ACT.Relu).then_inc(h_sb, 1)

                for kind, i in pe_steps:
                    if kind == "i":
                        slot_in(i)
                        if i == NS - 1:
                            act.wait_ge(gvar, n + 1)
                            nc.scalar.activation(gsd[:, :], gmv[:, :, 1], ACT.Sqrt, bias=eps[:, 0:1]).then_inc(gsd_r, 1)
                    elif kind == "u":
                        relu(i)
                        if i == 5:
                            act.wait_ge(lg_r, n + 1)
                            nc.scalar.activation(pe_[:, :, :], lg[:, :, :], ACT.Exp).then_inc(pe_r, 1)

            for k in range(NB):
                copy_xT(k)
            act.wait_ge(pool_set, 1)
            slots(0)

            def normalise(b):
                act.wait_ge(svar, b + 1)
                nc.scalar.activation(ssd[:, :], smv[:, :, 1], ACT.Sqrt, bias=eps[:, 0:1]).then_inc(ssd_r, 1)
                act.wait_ge(snb_r, b + 1)
                if b >= 2:
                    act.wait_ge(w_r, b - 1)
                    act.wait_ge(uT_ps, b - 1)
                for c in range(TB):
                    ins = nc.scalar.activation(u[:, b % 2, c, :], x[:, b * TB + c, :], ACT.Identity,
                                               bias=snb[:, b % 2, c:c + 1], scale=srs[:, b % 2, c:c + 1])
                ins.then_inc(u_r, 1)
                act.wait_ge(uT_ps, b + 1)
                if b >= 2:
                    act.wait_ge(v_ps, b - 1)
                nc.scalar.copy(uT[:, b % 2, :], bank[0][:, :]).then_inc(uT_sb, 1)

            normalise(0)
            for b in range(NB):
                act.wait_ge(v_ps, b + 1)
                if b >= 1:
                    act.wait_ge(vb_r, b)
                nc.scalar.copy(vq[:, :], bank[5][:, :]).then_inc(vq_sb, 1)
                if b + 1 < NB:
                    normalise(b + 1)
                if b >= 2:
                    copy_xT(NB + b - 2)
            copy_xT(2 * NB - 2)
            copy_xT(2 * NB - 1)
            slots(1)

        @block.vector
        def _(dve):
            links = [0]

            def link(ins):
                links[0] += 1
                ins.then_inc(dve_chain, 1)
                dve.wait_ge(dve_chain, links[0])

            V = nc.vector
            dve.wait_ge(omega_ps, 1)
            link(V.tensor_copy(om[:, 0:1], bank[7][:, 0:1]))
            link(V.tensor_tensor(om[:, 1:2], om[:, 0:1], om[:, 0:1], ALU.mult))
            link(V.tensor_scalar(om[:, 2:3], om[:, 1:2], 1.0, None, ALU.add))
            link(V.reciprocal(om[:, 3:4], om[:, 2:3]))
            link(V.tensor_scalar(om[:, 2:3], om[:, 1:2], -1.0, 1.0, ALU.mult, ALU.add))
            V.memset(ct[:, 0:1], 1.0)
            V.memset(st[:, 0:1], 0.0)
            V.tensor_tensor(ct[:, 1:2], om[:, 2:3], om[:, 3:4], ALU.mult)
            link(V.scalar_tensor_tensor(st[:, 1:2], om[:, 0:1], -2.0, om[:, 3:4], ALU.mult, ALU.mult))
            dve.wait_ge(set_ps, 1)
            link(V.tensor_copy(gate_c[:, :], bank[5][:, 0:E]))
            V.tensor_copy(cwT[:, :], bank[6][:, 2 * P:3 * P])
            V.tensor_copy(bt[:, :], bank[6][:, 0:2 * P]).then_inc(set_sb, 1)
            n = 1
            while n < SEQ:
                V.tensor_scalar(tmp[:, 0, 0:n], st[:, 1:n + 1], st[:, n:n + 1], None, ALU.mult)
                link(V.tensor_scalar(tmp[:, 1, 0:n], ct[:, 1:n + 1], st[:, n:n + 1], None, ALU.mult))
                V.scalar_tensor_tensor(ct[:, n + 1:2 * n + 1], ct[:, 1:n + 1], ct[:, n:n + 1], tmp[:, 0, 0:n],
                                       ALU.mult, ALU.subtract)
                link(V.scalar_tensor_tensor(st[:, n + 1:2 * n + 1], st[:, 1:n + 1], ct[:, n:n + 1], tmp[:, 1, 0:n],
                                            ALU.mult, ALU.add))
                n *= 2
            dve.wait_ge(set_ps, 2)
            V.tensor_copy(g1[:, :], bank[6][:, 0:P])
            V.tensor_copy(g2[:, :], bank[6][:, P:2 * P]).then_inc(tables, 1)
            dve.wait_ge(pool_set, 1)

            def route(n):
                lt = bank[2][:, 0:NT * E].rearrange("p (t e) -> p t e", e=E)
                dve.wait_ge(logits, (n + 1) * NB)
                link(V.reduce_max(top[:, :], lt, axis=AX))
                link(V.tensor_tensor(is_top[:, :, :], lt, top[:, :].unsqueeze(2).broadcast_to([P, NT, E]), ALU.is_equal))
                link(V.tensor_tensor(key[:, :, :], is_top[:, :, :], rev.unsqueeze(1).broadcast_to([P, NT, E]), ALU.mult))
                link(V.reduce_max(top_key[:, :], key[:, :, :], axis=AX))
                link(V.tensor_tensor(chosen[:, :, :].rearrange("p e t -> p t e"), key[:, :, :],
                                     top_key[:, :].unsqueeze(2).broadcast_to([P, NT, E]), ALU.is_equal))
                V.tensor_tensor_scan(counted[:, :, :].rearrange("p e t -> p (e t)"),
                                     restart[:, :, :].rearrange("p e t -> p (e t)"),
                                     chosen[:, :, :].rearrange("p e t -> p (e t)"), 0.0,
                                     ALU.mult, ALU.add).then_inc(marked, 1)
                dve.wait_ge(ranked, n + 1)
                rank = bank[3][:, 0:NT * E].rearrange("p (e t) -> p e t", e=E)
                link(V.tensor_tensor(own_count[:, :, :], rank, chosen[:, :, :], ALU.mult))
                link(V.reduce_sum(count[:, :], own_count[:, :, :].rearrange("p e t -> p t e"), axis=AX))
                V.tensor_scalar(over[:, :], count[:, :], CAP + 0.5, SKIP, ALU.is_gt, ALU.mult)
                link(V.scalar_tensor_tensor(slot_f[:, :], top_key[:, :], -float(CAP), count[:, :], ALU.mult, ALU.add))
                link(V.scalar_tensor_tensor(slot_i[:, :], slot_f[:, :], float(SLOTS - 1), over[:, :], ALU.add, ALU.add))
                V.tensor_scalar(split_i[:, 0, :], slot_i[:, :], P - 1, None, ALU.bitwise_and)
                link(V.tensor_scalar(split_i[:, 1, :], slot_i[:, :], P.bit_length() - 1, None, ALU.logical_shift_right))
                link(V.tensor_copy(split_f[:, :, :], split_i[:, :, :]))
                link(V.tensor_tensor(hot_tile[:, :, :], split_f[:, 1, :].unsqueeze(2).broadcast_to([P, NT, NS]),
                                     iota_ns.unsqueeze(1).broadcast_to([P, NT, NS]), ALU.is_equal))
                V.tensor_scalar(hot_tok[:, :, 0, :], hot_tile[:, :, :], place1, None, ALU.mult)
                V.tensor_tensor(hot_tok[:, :, 1, :], hot_tile[:, :, :], tile_no.unsqueeze(2).broadcast_to([P, NT, NS]),
                                ALU.mult)
                for t in range(NT):
                    ins = V.tensor_scalar(hot_place[:, t, :], iota_bf[:, :], split_f[:, 0, t:t + 1], None, ALU.is_equal)
                    if t % 8 == 7:
                        ins.then_inc(hot, 1)
                dve.wait_ge(placed, n + 1)
                link(V.tensor_copy(found[:, :, :], bank[3][:, 256:256 + 2 * NS].rearrange("p (a t) -> p a t", a=2)))
                V.tensor_scalar(unfilled[:, :], found[:, 0, :], 0.5, SKIP, ALU.is_lt, ALU.mult)
                link(V.scalar_tensor_tensor(tok_f[:, :], found[:, 1, :], float(P), found[:, 0, :], ALU.mult, ALU.add))
                if n == 1:
                    dve.wait_ge(d_scatter, 16 * NS)
                V.scalar_tensor_tensor(tok[:, :], tok_f[:, :], -1.0, unfilled[:, :], ALU.add, ALU.add).then_inc(indexed, 1)

            def slots(n):
                def slot_in(j):
                    dve.wait_ge(d_gather[j], 16 * (n + 1))
                    link(V.bn_stats(gstat[:, j, :], xg[:, j, :]))
                    link(V.bn_aggr(gmv[:, j, :], gstat[:, j, :]))
                    ins = V.tensor_scalar(xc[:, j, :], xg[:, j, :], gmv[:, j, 0:1], None, ALU.subtract)
                    ins.then_inc(centered, 1)
                    if j == NS - 1:
                        V.memset(om[:, 0:1], 0.0).then_inc(gvar, 1)

                def half_prob():
                    dve.wait_ge(gsd_r, n + 1)
                    link(V.reciprocal(grs[:, :], gsd[:, :]))
                    dve.wait_ge(slot_logits, n + 1)
                    link(V.tensor_tensor(lg[:, :, :], bank[2][:, 0:NS * E].rearrange("p (t e) -> p t e", e=E),
                                         grs[:, :].unsqueeze(2).broadcast_to([P, NS, E]), ALU.mult))
                    link(V.reduce_max(lgx[:, :], lg[:, :, :], axis=AX))
                    V.tensor_tensor(lg[:, :, :], lg[:, :, :], lgx[:, :].unsqueeze(2).broadcast_to([P, NS, E]),
                                    ALU.subtract).then_inc(lg_r, 1)

                def half_prob_end():
                    dve.wait_ge(pe_r, n + 1)
                    link(V.reduce_sum(psm[:, :], pe_[:, :, :], axis=AX))
                    link(V.reciprocal(prc[:, :], psm[:, :]))
                    link(V.scalar_tensor_tensor(gscale[:, :], grs[:, :], 0.5, prc[:, :], ALU.mult, ALU.mult))

                ended = False
                for kind, i in dve_steps:
                    if kind == "i":
                        slot_in(i)
                    elif kind == "l":
                        half_prob()
                    elif kind == "d":
                        dve.wait_ge(eo_ps, n * E + i + 1)
                        V.tensor_copy(eoT[:, i * CAP:(i + 1) * CAP],
                                      bank[6 + i % 2][:, 0:CAP]).then_inc(eo_sb, 1)
                    else:
                        if not ended:
                            half_prob_end()
                            ended = True
                        dve.wait_ge(row_ps, n * NS + i + 1)
                        V.scalar_tensor_tensor(xnew[:, i, :], bank[2 + i % 2][:, 0:P],
                                               gscale[:, i:i + 1], xg[:, i, :], ALU.mult, ALU.add).then_inc(row_sb, 1)

            route(0)
            slots(0)

            def stats(b):
                dve.wait_ge(d_x1[b], 16)
                for c in range(TB):
                    ins = V.bn_stats(sstat[:, c, :], x[:, b * TB + c, :])
                link(ins)
                if b >= 1:
                    dve.wait_ge(ssd_r, b)
                for c in range(TB):
                    ins = V.bn_aggr(smv[:, c, :], sstat[:, c, :])
                ins.then_inc(svar, 1)

            def shift(b):
                dve.wait_ge(svar, b + 1)
                dve.wait_ge(ssd_r, b + 1)
                if b >= 2:
                    dve.wait_ge(u_r, b - 1)
                link(V.reciprocal(srs[:, b % 2, :], ssd[:, :]))
                V.scalar_tensor_tensor(snb[:, b % 2, :], smv[:, :, 0], -1.0, srs[:, b % 2, :],
                                       ALU.mult, ALU.mult).then_inc(snb_r, 1)

            stats(0)
            shift(0)
            for b in range(NB):
                if b + 1 < NB:
                    stats(b + 1)
                dve.wait_ge(v_ps, b + 1)
                V.tensor_tensor(va[:, :], bank[4][:, :], ct[:, 0:SEQ], ALU.mult).then_inc(va_r, 1)
                if b + 1 < NB:
                    shift(b + 1)
                dve.wait_ge(va_r, b + 1)
                dve.wait_ge(vb_r, b + 1)
                if b >= 1:
                    dve.wait_ge(zs_r, b)
                V.tensor_tensor_scan(z[:, :], va[:, :], vb[:, :], 0.0, ALU.add, ALU.add).then_inc(z_r, 1)
                dve.wait_ge(z_r, b + 1)
                if b >= 2:
                    dve.wait_ge(y_ps, b - 1)
                V.tensor_tensor(zc[:, b % 2, :], z[:, :], ct[:, 0:SEQ], ALU.mult).then_inc(zc_r, 1)
                if b >= 1:
                    add_back = b - 1
                    dve.wait_ge(y_ps, add_back + 1)
                    dve.wait_ge(w_r, add_back + 1)
                    V.tensor_tensor(x2[:, add_back * TB:(add_back + 1) * TB, :],
                                    bank[6 + add_back % 2][:, :].rearrange("p (c d) -> p c d", c=TB),
                                    w[:, add_back % 2, :, :], ALU.add).then_inc(x2_r, 1)
            dve.wait_ge(y_ps, NB)
            dve.wait_ge(w_r, NB)
            V.tensor_tensor(x2[:, (NB - 1) * TB:NB * TB, :], bank[6 + (NB - 1) % 2][:, :].rearrange("p (c d) -> p c d", c=TB),
                            w[:, (NB - 1) % 2, :, :], ALU.add).then_inc(x2_r, 1)
            route(1)
            slots(1)

        @block.tensor
        def _(pe):
            M = nc.tensor.matmul
            pe.wait_ge(d_early, 16)
            pe.wait_ge(d_par, 16)
            M(bank[7][:, 0:1], sines[0:P // 2, :], par[:, :], start=True, stop=True).then_inc(omega_ps, 1)
            pe.wait_ge(d_gate, 16)
            M(bank[5][:, 0:E], center, gate[:, :], start=True, stop=True)
            pe.wait_ge(d_late, 16)
            pe.wait_ge(d_bw, 16)
            pe.wait_ge(d_cw, 16)
            M(bank[6][:, 0:2 * P], bw[:, :], basis_in, start=True, stop=True)
            nc.tensor.transpose(bank[6][:, 2 * P:3 * P], cw[:, :], ident).then_inc(set_ps, 1)
            pe.wait_ge(set_sb, 1)
            M(bank[6][:, 0:P], basis_out, cwT[:, :], start=True, stop=True)
            M(bank[6][:, P:2 * P], basis_turned, cwT[:, :], start=True, stop=True).then_inc(set_ps, 1)

            def turn_x(k):
                src = x if k < NB else x2
                b = k % NB
                if k < NB:
                    pe.wait_ge(d_x[b], 16)
                    if k >= 2:
                        pe.wait_ge(xT_sb, k - 1)
                else:
                    pe.wait_ge(x2_r, b + 1)
                    pe.wait_ge(xT_sb, k)
                dst = bank[k % 2 if k < NB else 1]
                for c in range(TB):
                    ins = nc.tensor.transpose(dst[:, c * P:(c + 1) * P], src[:, b * TB + c, :], ident)
                ins.then_inc(xT_ps, 1)

            def gate_x(k):
                pe.wait_ge(xT_sb, k + 1)
                for c in range(TB):
                    t = (k % NB) * TB + c
                    ins = M(bank[2][:, t * E:(t + 1) * E], xT[:, k % 2, c * P:(c + 1) * P], gate_c[:, :],
                            start=True, stop=True)
                ins.then_inc(logits, 1)

            def rank_and_place(n):
                pe.wait_ge(marked, n + 1)
                q = bank[3][:, 0:NT * E]
                M(q, ones_bf[:, :], counted[:, :, :].rearrange("p e t -> p (e t)"), start=True, stop=False)
                M(q, tri_bf[:, :], chosen[:, :, :].rearrange("p e t -> p (e t)"), start=False, stop=True).then_inc(ranked, 1)
                for t in range(NT):
                    if t % 8 == 0:
                        pe.wait_ge(hot, n * (NT // 8) + t // 8 + 1)
                    ins = M(bank[3][:, 256:256 + 2 * NS], hot_place[:, t, :],
                            hot_tok[:, t, :, :].rearrange("p a t -> p (a t)"), start=(t == 0), stop=(t == NT - 1))
                ins.then_inc(placed, 1)

            def slots(n):
                for kind, i in pe_steps:
                    if kind == "i":
                        pe.wait_ge(centered, n * NS + i + 1)
                        if i >= 2:
                            pe.wait_ge(slotT_sb, n * NS + i - 1)
                        nc.tensor.transpose(bank[i % 2][:, 0:P], xc[:, i, :], ident)\
                            .then_inc(slotT_ps, 1)
                    elif kind == "l":
                        pe.wait_ge(slotT_sb, (n + 1) * NS)
                        pe.wait_ge(indexed, n + 1)
                        for j in range(NS):
                            ins = M(bank[2][:, j * E:(j + 1) * E], xcT[:, j * P:(j + 1) * P], gate[:, :],
                                    start=True, stop=True)
                        ins.then_inc(slot_logits, 1)
                    elif kind == "u":
                        if n == 0 and i % (E // 2) == 0:
                            pe.wait_ge(d_w1[i // (E // 2)], 16)
                        pe.wait_ge(slotT_sb, n * NS + tiles_before(i))
                        for half in range(2):
                            if i >= 1:
                                pe.wait_ge(h_sb, n * 2 * E + 2 * (i - 1) + half + 1)
                            for c in range(HC):
                                ch = half * HC + c
                                ins = M(bank[4 + half][:, c * CAP:(c + 1) * CAP],
                                        w1s[:, i, ch * P:(ch + 1) * P], xcT[:, i * CAP:(i + 1) * CAP],
                                        start=True, stop=True)
                            ins.then_inc(h_ps, 1)
                    elif kind == "d":
                        if n == 0 and i % (E // 2) == 0:
                            pe.wait_ge(d_w2[i // (E // 2)], 16 * (E // 2))
                        pe.wait_ge(h_sb, n * 2 * E + 2 * i + 2)
                        if i >= 2:
                            pe.wait_ge(eo_sb, n * E + i - 1)
                        for c in range(FC):
                            ins = M(bank[6 + i % 2][:, 0:CAP], w2s[:, i, c, :], hT[:, i % 2, c, :],
                                    start=(c == 0), stop=(c == FC - 1))
                        ins.then_inc(eo_ps, 1)
                    else:
                        pe.wait_ge(eo_sb, n * E + min(E, experts_before(i)))
                        if i == 0:
                            pe.wait_ge(lg_r, n + 1)
                        if i >= 2:
                            pe.wait_ge(row_sb, n * NS + i - 1)
                        nc.tensor.transpose(bank[2 + i % 2][:, 0:P], eoT[:, i * P:(i + 1) * P], ident)\
                            .then_inc(row_ps, 1)

            turn_x(0)
            for k in range(1, NB):
                turn_x(k)
                gate_x(k - 1)
            gate_x(NB - 1)
            pe.wait_ge(pool_set, 1)
            pe.wait_ge(tables, 1)
            rank_and_place(0)
            pe.wait_ge(xT_sb, NB)
            slots(0)

            def turn_u(b):
                pe.wait_ge(u_r, b + 1)
                if b >= 1:
                    pe.wait_ge(uT_sb, b)
                for c in range(TB):
                    ins = nc.tensor.transpose(bank[0][:, c * P:(c + 1) * P], u[:, b % 2, c, :], ident)
                ins.then_inc(uT_ps, 1)

            def read_out(b):
                pe.wait_ge(zc_r, b + 1)
                pe.wait_ge(zs_r, b + 1)
                if b >= 2:
                    pe.wait_ge(x2_r, b - 1)
                for c in range(TB):
                    cs = slice(c * P, (c + 1) * P)
                    M(bank[6 + b % 2][:, cs], zc[:, b % 2, cs], g1[:, :], start=True, stop=False)
                    ins = M(bank[6 + b % 2][:, cs], zs[:, b % 2, cs], g2[:, :], start=False, stop=True)
                ins.then_inc(y_ps, 1)

            pe.wait_ge(row_sb, NS)
            turn_u(0)
            for b in range(NB):
                pe.wait_ge(uT_sb, b + 1)
                if b >= 1:
                    pe.wait_ge(va_r, b)
                    pe.wait_ge(vq_sb, b)
                M(bank[4][:, :], bt[:, 0:P], uT[:, b % 2, :], start=True, stop=True)
                M(bank[5][:, :], bt[:, P:2 * P], uT[:, b % 2, :], start=True, stop=True).then_inc(v_ps, 1)
                if b >= 1:
                    read_out(b - 1)
                if b + 1 < NB:
                    turn_u(b + 1)
                if b >= 2:
                    turn_x(NB + b - 2)
                if b >= 3:
                    gate_x(NB + b - 3)
            turn_x(2 * NB - 2)
            gate_x(2 * NB - 3)
            read_out(NB - 1)
            gate_x(2 * NB - 2)
            turn_x(2 * NB - 1)
            gate_x(2 * NB - 1)
            rank_and_place(1)
            slots(1)


def shape_constants(np, P, E, NS, NT):
    n = np.arange(P)
    eye = np.eye(P)
    k = np.arange(P) % (P // 2)
    rows = np.arange(1, P + 1)
    sines = -2.0 * np.sin(2 * np.pi * ((rows[:, None] * k[None, :]) % P) / P)
    sines[P // 2 - 1:, :] = 0.0
    early = np.concatenate([
        eye, eye - 1.0 / P, sines, np.tile(n, (P, 1)),
        (n[:, None] <= n[None, :]).astype(float) - 1.0,
        np.tile(E - np.arange(E), (P, 1)), np.tile(np.arange(NS), (P, 1)), np.tile(np.arange(NT), (P, 1)),
        n[:, None] + 1.0], axis=1)
    q = np.arange(P // 2)
    cos = np.cos(2 * np.pi * ((n[:, None] * q[None, :]) % P) / P)
    sin = np.sin(2 * np.pi * ((n[:, None] * q[None, :]) % P) / P)
    alt = (-1.0) ** n
    re_in, im_in = cos, -sin
    im_in[:, 0] = alt
    re_out, im_out = 2.0 / P * cos, -2.0 / P * sin
    re_out[:, 0], im_out[:, 0] = 1.0 / P, alt / P
    late = np.concatenate([re_in, im_in, im_in, -re_in, re_out, im_out, im_out, -re_out], axis=1)
    return early.astype(np.float32), late.astype(np.float32)


def kernel(**inputs):
    import numpy as np
    import concourse.bacc as bacc
    from concourse.bass_utils import run_bass_kernel_spmd

    names = ["L0_attn_u", "L0_attn_a_params", "L0_attn_B_w", "L0_attn_C_w", "L0_attn_D",
             "L0_ffn_gate_w", "L0_ffn_w1", "L0_ffn_w2"]
    arrays = {f"in_{n}": np.ascontiguousarray(inputs[n]) for n in names}
    shape = arrays["in_L0_attn_u"].shape
    n_experts = arrays["in_L0_ffn_w1"].shape[0]
    arrays["const_early"], arrays["const_late"] = shape_constants(
        np, 128, n_experts, n_experts * 160 // 128, shape[0] * shape[1] // 128)
    nc = bacc.Bacc("TRN2", target_bir_lowering=False, num_devices=1)
    args = [nc.dram_tensor(n, a.shape, mybir.dt.from_np(a.dtype), kind="ExternalInput").ap()
            for n, a in arrays.items()]
    out = nc.dram_tensor("out", shape, mybir.dt.float32, kind="ExternalOutput").ap()
    macaron_moe_ssm_kernel(nc, *args, out)
    r = run_bass_kernel_spmd(nc, [arrays], core_ids=[0])
    return r.results[0]["out"]
```

```python
import concourse.bass as bass
from concourse import mybir
from contextlib import ExitStack


def macaron_moe_ssm_kernel(nc, x_in, x_turned, a_params, b_w, c_w_turned, d_skip, gate_w, w1, w2, const_early, const_late, out):
    F32, F16, BF16, I32, U32 = (mybir.dt.float32, mybir.dt.float16, mybir.dt.bfloat16, mybir.dt.int32,
                                mybir.dt.uint32)
    ALU, ACT, AX = mybir.AluOpType, mybir.ActivationFunctionType, mybir.AxisListType.X

    NB, SEQ, D = x_in.shape
    E, _, F = w1.shape
    P = 128
    T = NB * SEQ
    TB = SEQ // P
    NT = T // P
    CAP = 160
    SLOTS = E * CAP
    NS = SLOTS // P
    FC = F // P
    HC = FC // 2
    Q = 32
    NQ = SLOTS // Q
    PIECES = [[(0, NB // 2), (NB // 2, NB)], [(0, 3), (3, 6), (6, NB)]]
    HALF = NT // 2
    SKIP = 2.0 * T
    EPS = 1e-5

    ctx = ExitStack()
    with ctx:
        def sb(name, shape, dt=F32):
            return ctx.enter_context(nc.sbuf_tensor(name, shape, dt))

        def sem(name):
            return ctx.enter_context(nc.semaphore(name))

        bank = [ctx.enter_context(nc.psum_tensor(f"bank{i}", [P, 512], F32)) for i in range(8)]

        ce = sb("ce", [P, const_early.shape[1]])
        cl = sb("cl", [P, const_late.shape[1]])
        at = [0]

        def part(n):
            at[0] += n
            return ce[:, at[0] - n:at[0]]

        ident, center, sines = part(P), part(P), part(P)
        tri_less_one, rev, iota_q, iota_nq, token1 = part(P), part(E), part(Q), part(NQ), part(NT)
        basis_in, basis_out, basis_turned = cl[:, 0:2 * P], cl[:, 2 * P:3 * P], cl[:, 3 * P:4 * P]
        tri_bf = sb("tri_bf", [P, P], BF16)
        ones_bf = sb("ones_bf", [P, P], BF16)
        restart = [[sb(f"restart{n}_{k}", [P, E, (b1 - b0) * TB], BF16) for k, (b0, b1) in enumerate(PIECES[n])]
                   for n in range(2)]
        eps = sb("eps", [P, 1])
        par = sb("par", [P // 2, 1])
        bw = sb("bw", [P, D])
        cwT = sb("cwT", [P, D])
        dsk = sb("dsk", [P, D])
        gate = sb("gate", [P, E])
        gate_c = sb("gate_c", [P, Q])
        w1s = sb("w1s", [P, E, F])
        w2s = sb("w2s", [P, E, FC, D])
        xt = sb("xt", [P, T])
        x1 = sb("x1", [P, NT, D])
        x2 = sb("x2", [P, NT, D])
        xT = sb("xT", [P, 2, SEQ])
        lgT = sb("lgT", [P, 2, SEQ])
        top = sb("top", [P, NT])
        is_top = sb("is_top", [P, NT, E])
        key = sb("key", [P, NT, E])
        top_key = sb("top_key", [P, NT])
        chosen = [[sb(f"chosen{n}_{k}", [P, E, (b1 - b0) * TB], BF16) for k, (b0, b1) in enumerate(PIECES[n])]
                  for n in range(2)]
        counted = [[sb(f"counted{n}_{k}", [P, E, (b1 - b0) * TB], BF16) for k, (b0, b1) in enumerate(PIECES[n])]
                   for n in range(2)]
        own_count = sb("own_count", [P, E, NT])
        count = sb("count", [P, NT])
        over = sb("over", [P, NT])
        slot_f = sb("slot_f", [P, NT])
        slot_i = sb("slot_i", [P, NT], I32)
        split_i = sb("split_i", [P, 2, NT], I32)
        split_f = sb("split_f", [P, 2, NT])
        hot_place = sb("hot_place", [P, NT, Q], F16)
        hot_quad = sb("hot_quad", [P, NT, NQ], F16)
        hot_tok = sb("hot_tok", [P, NT, NQ], F16)
        found = sb("found", [Q, 2, NQ])
        unfilled = sb("unfilled", [Q, NQ])
        tok_lo = sb("tok_lo", [Q, NQ])
        tok_hi = sb("tok_hi", [Q, NQ])
        tok_f = sb("tok_f", [Q, NQ])
        tok = sb("tok", [P, NS], U32)
        xg = sb("xg", [P, NS, D])
        xc = sb("xc", [P, NS, D])
        xcT = sb("xcT", [P, SLOTS])
        gstat = sb("gstat", [P, NS, 6])
        gmv = sb("gmv", [P, NS, 2])
        gsd = sb("gsd", [P, NS])
        grs = sb("grs", [P, NS])
        lg = sb("lg", [P, NS, E])
        lgx = sb("lgx", [P, NS])
        pe_ = sb("prob_e", [P, NS, E])
        psm = sb("prob_sum", [P, NS])
        prc = sb("prob_rc", [P, NS])
        gscale = sb("gscale", [P, NS])
        hT = sb("hT", [P, 2, FC, CAP])
        eoT = sb("eoT", [P, SLOTS])
        xnew = sb("xnew", [P, NS, D])
        om = sb("om", [P, 4])
        ct = sb("ct", [P, SEQ + 1])
        st = sb("st", [P, SEQ + 1])
        tmp = sb("tmp", [P, 2, SEQ // 2])
        bt = sb("bt", [P, 2 * P])
        g1 = sb("g1", [P, D])
        g2 = sb("g2", [P, D])
        sstat = sb("sstat", [P, 2, TB, 6])
        smv = sb("smv", [P, 2, TB, 2])
        ssd = sb("ssd", [P, 2, TB])
        srs = sb("srs", [P, 2, TB])
        snb = sb("snb", [P, 2, TB])
        u = sb("u", [P, 2, TB, D])
        ud = sb("ud", [P, TB, D])
        w = sb("w", [P, 2, TB, D])
        uT = sb("uT", [P, 2, SEQ])
        vq = sb("vq", [P, SEQ])
        va = sb("va", [P, SEQ])
        vb = sb("vb", [P, SEQ])
        z = sb("z", [P, SEQ])
        zc = sb("zc", [P, 2, SEQ])
        zs = sb("zs", [P, 2, SEQ])

        x1_dram = nc.dram_tensor("x1_scratch", [T, D], F32, kind="Internal").ap()
        x_rows = x_in.rearrange("b s d -> (b s) d")
        out_rows = out.rearrange("b s d -> (b s) d")

        def tiles(rows, b):
            return rows[b * SEQ:(b + 1) * SEQ, :].rearrange("(c p) d -> p c d", p=P)

        d_early, d_late, d_gate, d_par, d_bw, d_cw, d_dsk = (sem(f"d_{n}") for n in
                                                             ("early", "late", "gate", "par", "bw", "cw", "dsk"))
        d_w1 = [sem(f"d_w1_{i}") for i in range(2)]
        d_w2 = [sem(f"d_w2_{i}") for i in range(2)]
        d_xt = [sem(f"d_xt{b}") for b in range(NB)]
        d_x1 = [sem(f"d_x1_{b}") for b in range(NB)]
        d_fill = sem("d_fill")
        d_gather = [sem(f"d_gather{j}") for j in range(NS)]
        d_scatter = sem("d_scatter")
        d_out = sem("d_out")
        pool_set, pool_chain, dve_chain = sem("pool_set"), sem("pool_chain"), sem("dve_chain")
        set_ps, set_sb = sem("set_ps"), sem("set_sb")
        gate_ps, gate_sb, omega_ps, tables = sem("gate_ps"), sem("gate_sb"), sem("omega_ps"), sem("tables")
        xT_ps, xT_sb, logits = sem("xT_ps"), sem("xT_sb"), sem("logits")
        lgT_ps, lgT_sb = sem("lgT_ps"), sem("lgT_sb")

        def piece(n, k):
            return n * len(PIECES[0]) + k
        marked, ranked, rank_read, hot, placed, indexed = (sem(n) for n in ("marked", "ranked", "rank_read", "hot",
                                                                            "placed", "indexed"))
        centered, slotT_ps, slotT_sb, slot_logits = (sem(n) for n in ("centered", "slotT_ps", "slotT_sb", "slot_logits"))
        gvar, gsd_r, lg_r, pe_r = (sem(n) for n in ("gvar", "gsd_r", "lg_r", "pe_r"))
        h_ps, h_sb, eo_ps, eo_sb, row_ps, row_sb = (sem(n) for n in ("h_ps", "h_sb", "eo_ps", "eo_sb", "row_ps", "row_sb"))
        svar, ssd_r, snb_r, u_r, ud_r, w_r = (sem(n) for n in ("svar", "ssd_r", "snb_r", "u_r", "ud_r", "w_r"))
        uT_ps, uT_sb, v_ps, vq_sb, va_r, vb_r, z_r = (sem(n) for n in ("uT_ps", "uT_sb", "v_ps", "vq_sb", "va_r", "vb_r", "z_r"))
        zc_r, zs_r, y_ps, x2_r = (sem(n) for n in ("zc_r", "zs_r", "y_ps", "x2_r"))

        def experts_before(j):
            return -(-(j + 1) * P // CAP)

        def tiles_before(e):
            return -(-(e + 1) * CAP // P)

        pe_steps = [(s[0], int(s[1])) for s in
                    "i0 i1 u0 i2 i3 u1 d0 l0 l1 l2 i4 i5 u2 l3 d1 i6 i7 u3 l4 l5 d2 i8 i9 u4 l6 l7 l8 l9 d3".split()]
        dve_steps = [(s[0], int(s[1])) for s in "i0 i1 i2 i3 i4 i5 i6 i7 d0 i8 i9 d1 l0 d2 d3".split()]
        pe_out = dve_out = 0
        for e in range(4, E + 1):
            if e < E:
                pe_steps += [("u", e + 1)] * (e + 1 < E) + [("d", e)]
            while pe_out < NS and experts_before(pe_out) <= e:
                pe_steps.append(("o", pe_out))
                pe_out += 1
        for e in range(4, E + 1):
            while dve_out < NS and experts_before(dve_out) <= e:
                dve_steps.append(("o", dve_out))
                dve_out += 1
                if dve_out == 2:
                    dve_steps.append(("d", 4))
            if 4 < e < E:
                dve_steps.append(("d", e))

        block = ctx.enter_context(nc.Block())

        @block.sync
        def _(sp):
            for b in range(NB):
                sp.dma_start(xt[:, b * SEQ:(b + 1) * SEQ], x_turned[:, b * SEQ:(b + 1) * SEQ]).then_inc(d_xt[b], 16)
            for i in range(2):
                h = slice(i * E // 2, (i + 1) * E // 2)
                sp.dma_start(w1s[:, h, :], w1[h].rearrange("e d f -> d e f")).then_inc(d_w1[i], 16)
                for e in range(i * E // 2, (i + 1) * E // 2):
                    sp.dma_start(w2s[:, e, :, :], w2[e].rearrange("(c p) d -> p c d", p=P)).then_inc(d_w2[i], 16)
            sp.dma_start(x1_dram, x_rows).then_inc(d_fill, 16)
            sp.wait_ge(d_fill, 16)
            sp.wait_ge(d_scatter, 16 * NS)
            for b in range(NB):
                sp.dma_start(x1[:, b * TB:(b + 1) * TB, :], tiles(x1_dram, b)).then_inc(d_x1[b], 16)
            for b in range(NB):
                sp.wait_ge(x2_r, b + 1)
                sp.dma_start(tiles(out_rows, b), x2[:, b * TB:(b + 1) * TB, :]).then_inc(d_out, 16)
            sp.wait_ge(d_out, 16 * NB)
            sp.wait_ge(d_scatter, 16 * NS * 2)

        @block.gpsimd
        def _(pool):
            links = [0]

            def link(ins):
                links[0] += 1
                ins.then_inc(pool_chain, 1)
                pool.wait_ge(pool_chain, links[0])

            nc.gpsimd.memset(ones_bf[:, :], 1.0)
            nc.gpsimd.memset(eps[:, :], EPS)
            for n in range(2):
                for mask in restart[n]:
                    link(nc.gpsimd.memset(mask[:, :, :], 1.0))
                    nc.gpsimd.memset(mask[:, :, 0:1], 0.0)
            pool.wait_ge(d_early, 16)
            nc.gpsimd.tensor_copy(tri_bf[:, :], tri_less_one).then_inc(pool_set, 1)
            nc.gpsimd.memset(xg[:, :, :], 0.0).then_inc(pool_set, 1)

            def gather(n):
                pool.wait_ge(indexed, n + 1)
                pool.wait_ge(pool_set, 2)
                if n == 1:
                    pool.wait_ge(d_out, 16 * NB)
                    pool.wait_ge(row_sb, NS)
                for j in range(NS):
                    pool.indirect_dma_start(xg[:, j, :], None, (x_rows, out_rows)[n],
                                            bass.IndirectOffsetOnAxis(ap=tok[:, j:j + 1], axis=0),
                                            bounds_check=T - 1, oob_is_err=False).then_inc(d_gather[j], 16)

            def scatter(n):
                if n == 0:
                    pool.wait_ge(d_fill, 16)
                for j in range(NS):
                    pool.wait_ge(row_sb, n * NS + j + 1)
                    pool.indirect_dma_start((x1_dram, out_rows)[n],
                                            bass.IndirectOffsetOnAxis(ap=tok[:, j:j + 1], axis=0),
                                            xnew[:, j, :], None,
                                            bounds_check=T - 1, oob_is_err=False).then_inc(d_scatter, 16)

            gather(0)
            scatter(0)
            pool.wait_ge(d_dsk, 16)
            pool.wait_ge(tables, 1)

            def skip_product(b):
                pool.wait_ge(u_r, b + 1)
                if b >= 1:
                    pool.wait_ge(w_r, b)
                nc.gpsimd.tensor_tensor(ud[:, :, :], u[:, b % 2, :, :],
                                        dsk[:, :].unsqueeze(1).broadcast_to([P, TB, D]), ALU.mult).then_inc(ud_r, 1)

            def skip_sum(b):
                pool.wait_ge(ud_r, b + 1)
                if b >= 2:
                    pool.wait_ge(x2_r, b - 1)
                nc.gpsimd.tensor_tensor(w[:, b % 2, :, :], ud[:, :, :], x1[:, b * TB:(b + 1) * TB, :],
                                        ALU.add).then_inc(w_r, 1)

            def turn_back(b):
                pool.wait_ge(vq_sb, b + 1)
                if b >= 1:
                    pool.wait_ge(z_r, b)
                nc.gpsimd.tensor_tensor(vb[:, :], vq[:, :], st[:, 0:SEQ], ALU.mult).then_inc(vb_r, 1)

            def turn_forth(b):
                pool.wait_ge(z_r, b + 1)
                if b >= 2:
                    pool.wait_ge(y_ps, b - 1)
                nc.gpsimd.tensor_tensor(zs[:, b % 2, :], z[:, :], st[:, 0:SEQ], ALU.mult).then_inc(zs_r, 1)

            for i in range(-1, NB):
                if i >= 0:
                    turn_back(i)
                if i + 1 < NB:
                    skip_product(i + 1)
                if i >= 0:
                    turn_forth(i)
                if i + 1 < NB:
                    skip_sum(i + 1)
            gather(1)
            scatter(1)

        @block.scalar
        def _(act):
            act.dma_start(gate[:, :], gate_w).then_inc(d_gate, 16)
            act.dma_start(ce[:, :], const_early).then_inc(d_early, 16)
            act.dma_start(par[:, :], a_params.rearrange("(n o) -> n o", o=1)).then_inc(d_par, 16)
            act.dma_start(bw[:, :], b_w).then_inc(d_bw, 16)
            act.dma_start(cwT[:, :], c_w_turned).then_inc(d_cw, 16)
            act.dma_start(dsk[:, :], d_skip.partition_broadcast(P)).then_inc(d_dsk, 16)
            act.dma_start(cl[:, :], const_late).then_inc(d_late, 16)

            act.wait_ge(pool_set, 1)
            nc.scalar.activation(gsd[:, 0:1], eps[:, 0:1], ACT.Sqrt)
            for k in range(len(PIECES[0])):
                act.wait_ge(lgT_ps, k + 1)
                nc.scalar.copy(lgT[:, k, :], bank[2 + k][:, :]).then_inc(lgT_sb, 1)
            act.wait_ge(set_ps, 1)
            nc.scalar.copy(g1[:, :], bank[4][:, 0:P])
            nc.scalar.copy(g2[:, :], bank[4][:, P:2 * P])
            nc.scalar.copy(bt[:, :], bank[6][:, 0:2 * P]).then_inc(tables, 1)

            def copy_xT(b):
                act.wait_ge(xT_ps, b + 1)
                if b >= 2:
                    act.wait_ge(logits, len(PIECES[0]) + b - 1)
                nc.scalar.copy(xT[:, b % 2, :], bank[1][:, :]).then_inc(xT_sb, 1)

            def slots(n):
                def slot_in(j):
                    act.wait_ge(slotT_ps, n * NS + j + 1)
                    nc.scalar.copy(xcT[:, j * P:(j + 1) * P],
                                   bank[j % 2][:, 0:P]).then_inc(slotT_sb, 1)

                def relu(e):
                    for half in range(2):
                        act.wait_ge(h_ps, n * 2 * E + 2 * e + half + 1)
                        if e >= 2:
                            act.wait_ge(eo_ps, n * E + e - 1)
                        nc.scalar.activation(hT[:, e % 2, half * HC:(half + 1) * HC, :],
                                             bank[4 + half][:, 0:HC * CAP]
                                             .rearrange("p (c s) -> p c s", c=HC), ACT.Relu).then_inc(h_sb, 1)

                for kind, i in pe_steps:
                    if kind == "i":
                        slot_in(i)
                        if i == NS - 1:
                            act.wait_ge(gvar, n + 1)
                            nc.scalar.activation(gsd[:, :], gmv[:, :, 1], ACT.Sqrt, bias=eps[:, 0:1]).then_inc(gsd_r, 1)
                    elif kind == "u":
                        relu(i)
                        if i == 4:
                            act.wait_ge(lg_r, n + 1)
                            nc.scalar.activation(pe_[:, :, :], lg[:, :, :], ACT.Exp).then_inc(pe_r, 1)

            slots(0)

            def deviation(b):
                act.wait_ge(svar, b + 1)
                if b >= 2:
                    act.wait_ge(snb_r, b - 1)
                nc.scalar.activation(ssd[:, b % 2, :], smv[:, b % 2, :, 1], ACT.Sqrt, bias=eps[:, 0:1]).then_inc(ssd_r, 1)

            def normalise(b):
                act.wait_ge(snb_r, b + 1)
                if b >= 2:
                    act.wait_ge(ud_r, b - 1)
                    act.wait_ge(uT_ps, b - 1)
                for c in range(TB):
                    ins = nc.scalar.activation(u[:, b % 2, c, :], x1[:, b * TB + c, :], ACT.Identity,
                                               bias=snb[:, b % 2, c:c + 1], scale=srs[:, b % 2, c:c + 1])
                ins.then_inc(u_r, 1)

            for i in range(-2, NB + 2):
                if 0 <= i < NB:
                    act.wait_ge(v_ps, i + 1)
                    if i >= 1:
                        act.wait_ge(vb_r, i)
                    nc.scalar.copy(vq[:, :], bank[5][:, :]).then_inc(vq_sb, 1)
                if i + 2 < NB:
                    deviation(i + 2)
                if 0 <= i + 1 < NB:
                    act.wait_ge(uT_ps, i + 2)
                    if i >= 1:
                        act.wait_ge(v_ps, i)
                    nc.scalar.copy(uT[:, (i + 1) % 2, :], bank[0][:, :]).then_inc(uT_sb, 1)
                if i + 2 < NB:
                    normalise(i + 2)
                if 0 <= i - 1 < NB:
                    copy_xT(i - 1)
            slots(1)

        @block.vector
        def _(dve):
            links = [0]

            def link(ins):
                links[0] += 1
                ins.then_inc(dve_chain, 1)
                dve.wait_ge(dve_chain, links[0])

            V = nc.vector
            link(V.memset(gate_c[:, :], 0.0))
            dve.wait_ge(gate_ps, 1)
            V.tensor_copy(gate_c[:, 0:E], bank[5][:, 0:E]).then_inc(gate_sb, 1)
            dve.wait_ge(omega_ps, 1)
            link(V.tensor_copy(om[:, 0:1], bank[7][:, 0:1]))
            link(V.tensor_tensor(om[:, 1:2], om[:, 0:1], om[:, 0:1], ALU.mult))
            link(V.tensor_scalar(om[:, 2:3], om[:, 1:2], 1.0, None, ALU.add))
            link(V.reciprocal(om[:, 3:4], om[:, 2:3]))
            link(V.tensor_scalar(om[:, 2:3], om[:, 1:2], -1.0, 1.0, ALU.mult, ALU.add))
            V.memset(ct[:, 0:1], 1.0)
            V.memset(st[:, 0:1], 0.0)
            V.tensor_tensor(ct[:, 1:2], om[:, 2:3], om[:, 3:4], ALU.mult)
            link(V.scalar_tensor_tensor(st[:, 1:2], om[:, 0:1], -2.0, om[:, 3:4], ALU.mult, ALU.mult))
            def powers(first, last):
                for level in range(first, last):
                    m = 1 << level
                    V.tensor_scalar(tmp[:, 0, 0:m], st[:, 1:m + 1], st[:, m:m + 1], None, ALU.mult)
                    link(V.tensor_scalar(tmp[:, 1, 0:m], ct[:, 1:m + 1], st[:, m:m + 1], None, ALU.mult))
                    V.scalar_tensor_tensor(ct[:, m + 1:2 * m + 1], ct[:, 1:m + 1], ct[:, m:m + 1], tmp[:, 0, 0:m],
                                           ALU.mult, ALU.subtract)
                    link(V.scalar_tensor_tensor(st[:, m + 1:2 * m + 1], st[:, 1:m + 1], ct[:, m:m + 1],
                                                tmp[:, 1, 0:m], ALU.mult, ALU.add))

            def mark(n, k):
                b0, b1 = PIECES[n][k]
                nb, wd = b1 - b0, (b1 - b0) * TB
                ts = slice(b0 * TB, b1 * TB)

                def by_batch(a):
                    return a.rearrange("p (b c) e -> p b c e", c=TB)

                def over_experts(a):
                    return by_batch(a.unsqueeze(2).broadcast_to([P, wd, E]))

                if n == 0:
                    lt = bank[2 + k % 2][:, 0:TB * nb * Q].rearrange("p (c b q) -> p b c q", b=nb, q=Q)[:, :, :, 0:E]
                    dve.wait_ge(logits, k + 1)
                else:
                    lt = by_batch(bank[2 + k % 2][:, 0:wd * E].rearrange("p (t e) -> p t e", e=E))
                    dve.wait_ge(logits, len(PIECES[0]) + b1)
                link(V.reduce_max(top[:, ts].rearrange("p (b c) -> p b c", c=TB), lt, axis=AX))
                link(V.tensor_tensor(by_batch(is_top[:, ts, :]), lt, over_experts(top[:, ts]), ALU.is_equal))
                link(V.tensor_tensor(key[:, ts, :], is_top[:, ts, :], rev.unsqueeze(1).broadcast_to([P, wd, E]), ALU.mult))
                link(V.reduce_max(top_key[:, ts], key[:, ts, :], axis=AX))
                link(V.tensor_tensor(chosen[n][k][:, :, :].rearrange("p e t -> p t e"), key[:, ts, :],
                                     top_key[:, ts].unsqueeze(2).broadcast_to([P, wd, E]), ALU.is_equal))
                V.tensor_tensor_scan(counted[n][k][:, :, :].rearrange("p e t -> p (e t)"),
                                     restart[n][k][:, :, :].rearrange("p e t -> p (e t)"),
                                     chosen[n][k][:, :, :].rearrange("p e t -> p (e t)"), 0.0,
                                     ALU.mult, ALU.add).then_inc(marked, 1)

            def make_hot(n, k):
                b0, b1 = PIECES[n][k]
                wd = (b1 - b0) * TB
                ts = slice(b0 * TB, b1 * TB)
                dve.wait_ge(ranked, piece(n, k) + 1)
                rank = bank[2 + k % 2][:, 0:wd * E].rearrange("p (e t) -> p e t", e=E)
                V.tensor_tensor(own_count[:, :, ts], rank, chosen[n][k][:, :, :], ALU.mult).then_inc(rank_read, 1)
                dve.wait_ge(rank_read, piece(n, k) + 1)
                link(V.reduce_sum(count[:, ts], own_count[:, :, ts].rearrange("p e t -> p t e"), axis=AX))
                V.tensor_scalar(over[:, ts], count[:, ts], CAP + 0.5, SKIP, ALU.is_gt, ALU.mult)
                link(V.scalar_tensor_tensor(slot_f[:, ts], top_key[:, ts], -float(CAP), count[:, ts], ALU.mult, ALU.add))
                link(V.scalar_tensor_tensor(slot_i[:, ts], slot_f[:, ts], float(SLOTS - 1), over[:, ts], ALU.add, ALU.add))
                V.tensor_scalar(split_i[:, 0, ts], slot_i[:, ts], Q - 1, None, ALU.bitwise_and)
                link(V.tensor_scalar(split_i[:, 1, ts], slot_i[:, ts], Q.bit_length() - 1, None, ALU.logical_shift_right))
                link(V.tensor_copy(split_f[:, :, ts], split_i[:, :, ts]))
                link(V.tensor_tensor(hot_quad[:, ts, :], split_f[:, 1, ts].unsqueeze(2).broadcast_to([P, wd, NQ]),
                                     iota_nq.unsqueeze(1).broadcast_to([P, wd, NQ]), ALU.is_equal))
                V.tensor_tensor(hot_place[:, ts, :], split_f[:, 0, ts].unsqueeze(2).broadcast_to([P, wd, Q]),
                                iota_q.unsqueeze(1).broadcast_to([P, wd, Q]), ALU.is_equal)
                V.tensor_tensor(hot_tok[:, ts, :], hot_quad[:, ts, :],
                                token1[:, ts].unsqueeze(2).broadcast_to([P, wd, NQ]), ALU.mult).then_inc(hot, 1)

            def index(n):
                dve.wait_ge(placed, n + 1)
                link(V.tensor_copy(found[:, :, :], bank[7][0:Q, 0:2 * NQ].rearrange("p (a t) -> p a t", a=2)))
                V.tensor_tensor(tok_lo[:, :], found[:, 0, :], found[:, 1, :], ALU.add)
                link(V.tensor_scalar(tok_hi[:, :], found[:, 1, :], 0.5, float(HALF * P), ALU.is_gt, ALU.mult))
                V.tensor_scalar(unfilled[:, :], tok_lo[:, :], 0.5, SKIP, ALU.is_lt, ALU.mult)
                link(V.tensor_tensor(tok_f[:, :], tok_lo[:, :], tok_hi[:, :], ALU.add))
                if n == 1:
                    dve.wait_ge(d_scatter, 16 * NS)
                for r in range(P // Q):
                    ins = V.scalar_tensor_tensor(tok[r * Q:(r + 1) * Q, :], tok_f[:, r::P // Q], -1.0,
                                                 unfilled[:, r::P // Q], ALU.add, ALU.add)
                ins.then_inc(indexed, 1)

            def slots(n):
                def slot_in(j):
                    dve.wait_ge(d_gather[j], 16 * (n + 1))
                    link(V.bn_stats(gstat[:, j, :], xg[:, j, :]))
                    link(V.bn_aggr(gmv[:, j, :], gstat[:, j, :]))
                    ins = V.tensor_scalar(xc[:, j, :], xg[:, j, :], gmv[:, j, 0:1], None, ALU.subtract)
                    ins.then_inc(centered, 1)
                    if j == NS - 1:
                        V.memset(om[:, 0:1], 0.0).then_inc(gvar, 1)

                def half_prob():
                    dve.wait_ge(gsd_r, n + 1)
                    link(V.reciprocal(grs[:, :], gsd[:, :]))
                    dve.wait_ge(slot_logits, n + 1)
                    link(V.tensor_tensor(lg[:, :, :], bank[2][:, 0:NS * E].rearrange("p (t e) -> p t e", e=E),
                                         grs[:, :].unsqueeze(2).broadcast_to([P, NS, E]), ALU.mult))
                    link(V.reduce_max(lgx[:, :], lg[:, :, :], axis=AX))
                    V.tensor_tensor(lg[:, :, :], lg[:, :, :], lgx[:, :].unsqueeze(2).broadcast_to([P, NS, E]),
                                    ALU.subtract).then_inc(lg_r, 1)

                def half_prob_end():
                    dve.wait_ge(pe_r, n + 1)
                    link(V.reduce_sum(psm[:, :], pe_[:, :, :], axis=AX))
                    link(V.reciprocal(prc[:, :], psm[:, :]))
                    link(V.scalar_tensor_tensor(gscale[:, :], grs[:, :], 0.5, prc[:, :], ALU.mult, ALU.mult))

                ended = False
                for kind, i in dve_steps:
                    if kind == "i":
                        slot_in(i)
                    elif kind == "l":
                        half_prob()
                    elif kind == "d":
                        dve.wait_ge(eo_ps, n * E + i + 1)
                        V.tensor_copy(eoT[:, i * CAP:(i + 1) * CAP], bank[6 + i % 2][:, 0:CAP]).then_inc(eo_sb, 1)
                        if n == 0 and 5 <= i < 8:
                            powers(i + 1, i + 2)
                    else:
                        if not ended:
                            half_prob_end()
                            ended = True
                        dve.wait_ge(row_ps, n * NS + i + 1)
                        V.scalar_tensor_tensor(xnew[:, i, :], bank[2 + i % 2][:, 0:P],
                                               gscale[:, i:i + 1], xg[:, i, :], ALU.mult, ALU.add).then_inc(row_sb, 1)

            powers(0, 3)
            dve.wait_ge(pool_set, 1)
            for k in range(len(PIECES[0])):
                mark(0, k)
                make_hot(0, k)
            index(0)
            powers(3, 6)
            slots(0)

            def stats(b):
                dve.wait_ge(d_x1[b], 16)
                for c in range(TB):
                    ins = V.bn_stats(sstat[:, b % 2, c, :], x1[:, b * TB + c, :])
                link(ins)
                if b >= 2:
                    dve.wait_ge(ssd_r, b - 1)
                for c in range(TB):
                    ins = V.bn_aggr(smv[:, b % 2, c, :], sstat[:, b % 2, c, :])
                ins.then_inc(svar, 1)

            def shift(b):
                dve.wait_ge(svar, b + 1)
                dve.wait_ge(ssd_r, b + 1)
                if b >= 2:
                    dve.wait_ge(u_r, b - 1)
                link(V.reciprocal(srs[:, b % 2, :], ssd[:, b % 2, :]))
                V.scalar_tensor_tensor(snb[:, b % 2, :], smv[:, b % 2, :, 0], -1.0, srs[:, b % 2, :],
                                       ALU.mult, ALU.mult).then_inc(snb_r, 1)

            def add_back(b):
                dve.wait_ge(y_ps, b + 1)
                dve.wait_ge(w_r, b + 1)
                V.tensor_tensor(x2[:, b * TB:(b + 1) * TB, :], bank[6][:, :].rearrange("p (c d) -> p c d", c=TB),
                                w[:, b % 2, :, :], ALU.add).then_inc(x2_r, 1)

            for i in range(-2, NB + 1):
                if 0 <= i < NB:
                    dve.wait_ge(v_ps, i + 1)
                    V.tensor_tensor(va[:, :], bank[4][:, :], ct[:, 0:SEQ], ALU.mult).then_inc(va_r, 1)
                if i + 2 < NB:
                    stats(i + 2)
                if i >= 1:
                    add_back(i - 1)
                if i + 2 < NB:
                    shift(i + 2)
                if 0 <= i < NB:
                    dve.wait_ge(va_r, i + 1)
                    dve.wait_ge(vb_r, i + 1)
                    if i >= 1:
                        dve.wait_ge(zs_r, i)
                    V.tensor_tensor_scan(z[:, :], va[:, :], vb[:, :], 0.0, ALU.add, ALU.add).then_inc(z_r, 1)
                    dve.wait_ge(z_r, i + 1)
                    if i >= 2:
                        dve.wait_ge(y_ps, i - 1)
                    V.tensor_tensor(zc[:, i % 2, :], z[:, :], ct[:, 0:SEQ], ALU.mult).then_inc(zc_r, 1)
                for k, (_, b1) in enumerate(PIECES[1][:-1]):
                    if i == b1 + 1:
                        mark(1, k)
                    if i == b1 + 2:
                        make_hot(1, k)
            mark(1, len(PIECES[1]) - 1)
            make_hot(1, len(PIECES[1]) - 1)
            index(1)
            slots(1)

        @block.tensor
        def _(pe):
            M = nc.tensor.matmul
            pe.wait_ge(d_early, 16)
            pe.wait_ge(d_gate, 16)
            M(bank[5][:, 0:E], center, gate[:, :], start=True, stop=True).then_inc(gate_ps, 1)
            pe.wait_ge(d_par, 16)
            M(bank[7][:, 0:1], sines[0:P // 2, :], par[:, :], start=True, stop=True).then_inc(omega_ps, 1)

            def turn_x2(b):
                pe.wait_ge(x2_r, b + 1)
                if b >= 1:
                    pe.wait_ge(xT_sb, b)
                for c in range(TB):
                    ins = nc.tensor.transpose(bank[1][:, c * P:(c + 1) * P], x2[:, b * TB + c, :], ident)
                ins.then_inc(xT_ps, 1)

            def gate_turned(k):
                b0, b1 = PIECES[0][k]
                for b in range(b0, b1):
                    pe.wait_ge(d_xt[b], 16)
                    ins = M(bank[2 + k][(b - b0) * Q:(b - b0 + 1) * Q, :], gate_c[:, :], xt[:, b * SEQ:(b + 1) * SEQ],
                            start=True, stop=True)
                ins.then_inc(lgT_ps, 1)

            def turn_logits(k):
                pe.wait_ge(lgT_sb, k + 1)
                for c in range(TB):
                    ins = nc.tensor.transpose(bank[2 + k][:, c * P:(c + 1) * P], lgT[:, k, c * P:(c + 1) * P], ident)
                ins.then_inc(logits, 1)

            def gate_x2(b):
                k = [b0 <= b < b1 for b0, b1 in PIECES[1]].index(True)
                pe.wait_ge(xT_sb, b + 1)
                if k >= 2 and b == PIECES[1][k][0]:
                    pe.wait_ge(rank_read, piece(1, k - 2) + 1)
                for c in range(TB):
                    t = (b - PIECES[1][k][0]) * TB + c
                    ins = M(bank[2 + k % 2][:, t * E:(t + 1) * E], xT[:, b % 2, c * P:(c + 1) * P], gate_c[:, 0:E],
                            start=True, stop=True)
                ins.then_inc(logits, 1)

            def rank(n, k):
                wd = (PIECES[n][k][1] - PIECES[n][k][0]) * TB
                pe.wait_ge(marked, piece(n, k) + 1)
                q = bank[2 + k % 2][:, 0:wd * E].rearrange("p (e t) -> p e t", e=E)
                for before in range(k):
                    last = (PIECES[n][before][1] - PIECES[n][before][0]) * TB - 1
                    M(q, ones_bf[:, :], counted[n][before][:, :, last:last + 1].broadcast_to([P, E, wd]),
                      start=(before == 0), stop=False)
                M(q, ones_bf[:, :], counted[n][k][:, :, :], start=(k == 0), stop=False)
                M(q, tri_bf[:, :], chosen[n][k][:, :, :], start=False, stop=True).then_inc(ranked, 1)

            def place(n, k):
                pe.wait_ge(hot, piece(n, k) + 1)
                for t in range(PIECES[n][k][0] * TB, PIECES[n][k][1] * TB):
                    h = t // HALF
                    ins = M(bank[7][0:Q, h * NQ:(h + 1) * NQ], hot_place[:, t, :], hot_tok[:, t, :],
                            start=(t % HALF == 0), stop=(t % HALF == HALF - 1))
                if k == len(PIECES[n]) - 1:
                    ins.then_inc(placed, 1)

            def slots(n):
                for kind, i in pe_steps:
                    if kind == "i":
                        pe.wait_ge(centered, n * NS + i + 1)
                        if i >= 2:
                            pe.wait_ge(slotT_sb, n * NS + i - 1)
                        nc.tensor.transpose(bank[i % 2][:, 0:P], xc[:, i, :], ident)\
                            .then_inc(slotT_ps, 1)
                    elif kind == "l":
                        pe.wait_ge(slotT_sb, n * NS + i + 1)
                        pe.wait_ge(indexed, n + 1)
                        ins = M(bank[2][:, i * E:(i + 1) * E], xcT[:, i * P:(i + 1) * P], gate[:, :], start=True, stop=True)
                        if i == NS - 1:
                            ins.then_inc(slot_logits, 1)
                    elif kind == "u":
                        if n == 0 and i % (E // 2) == 0:
                            pe.wait_ge(d_w1[i // (E // 2)], 16)
                        pe.wait_ge(slotT_sb, n * NS + tiles_before(i))
                        for half in range(2):
                            if i >= 1:
                                pe.wait_ge(h_sb, n * 2 * E + 2 * (i - 1) + half + 1)
                            for c in range(HC):
                                ch = half * HC + c
                                ins = M(bank[4 + half][:, c * CAP:(c + 1) * CAP],
                                        w1s[:, i, ch * P:(ch + 1) * P], xcT[:, i * CAP:(i + 1) * CAP],
                                        start=True, stop=True)
                            ins.then_inc(h_ps, 1)
                    elif kind == "d":
                        if n == 0 and i % (E // 2) == 0:
                            pe.wait_ge(d_w2[i // (E // 2)], 16 * (E // 2))
                        pe.wait_ge(h_sb, n * 2 * E + 2 * i + 2)
                        if i >= 2:
                            pe.wait_ge(eo_sb, n * E + i - 1)
                        for c in range(FC):
                            ins = M(bank[6 + i % 2][:, 0:CAP], w2s[:, i, c, :], hT[:, i % 2, c, :],
                                    start=(c == 0), stop=(c == FC - 1))
                        ins.then_inc(eo_ps, 1)
                    else:
                        pe.wait_ge(eo_sb, n * E + min(E, experts_before(i)))
                        if i == 0:
                            pe.wait_ge(lg_r, n + 1)
                        if i >= 2:
                            pe.wait_ge(row_sb, n * NS + i - 1)
                        nc.tensor.transpose(bank[2 + i % 2][:, 0:P], eoT[:, i * P:(i + 1) * P], ident)\
                            .then_inc(row_ps, 1)

            pe.wait_ge(gate_sb, 1)
            gate_turned(0)
            gate_turned(1)
            turn_logits(0)
            turn_logits(1)
            pe.wait_ge(pool_set, 1)
            rank(0, 0)
            pe.wait_ge(d_late, 16)
            pe.wait_ge(d_bw, 16)
            pe.wait_ge(d_cw, 16)
            M(bank[6][:, 0:2 * P], bw[:, :], basis_in, start=True, stop=True)
            M(bank[4][:, 0:P], basis_out, cwT[:, :], start=True, stop=True)
            M(bank[4][:, P:2 * P], basis_turned, cwT[:, :], start=True, stop=True).then_inc(set_ps, 1)
            place(0, 0)
            rank(0, 1)
            place(0, 1)
            pe.wait_ge(tables, 1)
            slots(0)

            def turn_u(b):
                pe.wait_ge(u_r, b + 1)
                if b >= 1:
                    pe.wait_ge(uT_sb, b)
                for c in range(TB):
                    ins = nc.tensor.transpose(bank[0][:, c * P:(c + 1) * P], u[:, b % 2, c, :], ident)
                ins.then_inc(uT_ps, 1)

            def read_out(b):
                pe.wait_ge(zc_r, b + 1)
                pe.wait_ge(zs_r, b + 1)
                if b >= 1:
                    pe.wait_ge(x2_r, b)
                for c in range(TB):
                    cs = slice(c * P, (c + 1) * P)
                    M(bank[6][:, cs], zc[:, b % 2, cs], g1[:, :], start=True, stop=False)
                    ins = M(bank[6][:, cs], zs[:, b % 2, cs], g2[:, :], start=False, stop=True)
                ins.then_inc(y_ps, 1)

            pe.wait_ge(row_sb, NS)
            turn_u(0)
            for i in range(NB + 2):
                if i < NB:
                    pe.wait_ge(uT_sb, i + 1)
                    if i >= 1:
                        pe.wait_ge(va_r, i)
                        pe.wait_ge(vq_sb, i)
                    M(bank[4][:, :], bt[:, 0:P], uT[:, i % 2, :], start=True, stop=True)
                    M(bank[5][:, :], bt[:, P:2 * P], uT[:, i % 2, :], start=True, stop=True).then_inc(v_ps, 1)
                if 0 <= i - 1 < NB:
                    read_out(i - 1)
                if i + 1 < NB:
                    turn_u(i + 1)
                for k, (_, b1) in enumerate(PIECES[1][:-1]):
                    if i == b1 + 2:
                        rank(1, k)
                    if i == b1 + 3:
                        place(1, k)
                if 0 <= i - 2 < NB:
                    gate_x2(i - 2)
                if 0 <= i - 1 < NB:
                    turn_x2(i - 1)
            rank(1, len(PIECES[1]) - 1)
            place(1, len(PIECES[1]) - 1)
            slots(1)


def shape_constants(np, P, E, NQ, NT):
    n = np.arange(P)
    eye = np.eye(P)
    k = np.arange(P) % (P // 2)
    rows = np.arange(1, P + 1)
    sines = -2.0 * np.sin(2 * np.pi * ((rows[:, None] * k[None, :]) % P) / P)
    sines[P // 2 - 1:, :] = 0.0
    early = np.concatenate([
        eye, eye - 1.0 / P, sines,
        (n[:, None] <= n[None, :]).astype(float) - 1.0,
        np.tile(E - np.arange(E), (P, 1)), np.tile(np.arange(32), (P, 1)), np.tile(np.arange(NQ), (P, 1)), (np.arange(NT)[None, :] % (NT // 2)) * P + n[:, None] + 1.0], axis=1)
    q = np.arange(P // 2)
    cos = np.cos(2 * np.pi * ((n[:, None] * q[None, :]) % P) / P)
    sin = np.sin(2 * np.pi * ((n[:, None] * q[None, :]) % P) / P)
    alt = (-1.0) ** n
    re_in, im_in = cos, -sin
    im_in[:, 0] = alt
    re_out, im_out = 2.0 / P * cos, -2.0 / P * sin
    re_out[:, 0], im_out[:, 0] = 1.0 / P, alt / P
    late = np.concatenate([re_in, im_in, im_in, -re_in, re_out, im_out, im_out, -re_out], axis=1)
    return early.astype(np.float32), late.astype(np.float32)


def kernel(**inputs):
    import numpy as np
    import concourse.bacc as bacc
    from concourse.bass_utils import run_bass_kernel_spmd

    ins = {n: np.ascontiguousarray(inputs[n]) for n in (
        "L0_attn_u", "L0_attn_a_params", "L0_attn_B_w", "L0_attn_C_w", "L0_attn_D", "L0_ffn_gate_w", "L0_ffn_w1", "L0_ffn_w2")}
    x = ins["L0_attn_u"]
    shape, n_experts = x.shape, ins["L0_ffn_w1"].shape[0]
    early, late = shape_constants(np, 128, n_experts, n_experts * 160 // 32, shape[0] * shape[1] // 128)
    arrays = {
        "x": x, "x_turned": np.ascontiguousarray(x.reshape(-1, shape[2]).T), "a_params": ins["L0_attn_a_params"],
        "b_w": ins["L0_attn_B_w"], "c_w_turned": np.ascontiguousarray(ins["L0_attn_C_w"].T), "d_skip": ins["L0_attn_D"],
        "gate_w": ins["L0_ffn_gate_w"], "w1": ins["L0_ffn_w1"], "w2": ins["L0_ffn_w2"],
        "const_early": early, "const_late": late}
    nc = bacc.Bacc("TRN2", target_bir_lowering=False, num_devices=1)
    args = [nc.dram_tensor(n, a.shape, mybir.dt.from_np(a.dtype), kind="ExternalInput").ap()
            for n, a in arrays.items()]
    out = nc.dram_tensor("out", shape, mybir.dt.float32, kind="ExternalOutput").ap()
    macaron_moe_ssm_kernel(nc, *args, out)
    r = run_bass_kernel_spmd(nc, [arrays], core_ids=[0])
    return r.results[0]["out"]
```

```python
import concourse.bass as bass
from concourse import mybir
from contextlib import ExitStack


def macaron_moe_ssm_kernel(nc, x_in, x_turned, a_params, b_w, c_w_turned, d_skip, gate_w, w1, w2,
                           const_center, const_early, const_late, out):
    F32, F16, BF16, I16, I32, U32 = (mybir.dt.float32, mybir.dt.float16, mybir.dt.bfloat16, mybir.dt.int16,
                                     mybir.dt.int32, mybir.dt.uint32)
    ALU, ACT, AX = mybir.AluOpType, mybir.ActivationFunctionType, mybir.AxisListType.X

    NB, SEQ, D = x_in.shape
    E, _, F = w1.shape
    P = 128
    T = NB * SEQ
    TB = SEQ // P
    NT = T // P
    CAP = 160
    SLOTS = E * CAP
    NS = SLOTS // P
    FC = F // P
    HC = FC // 2
    Q = 32
    SW = 64
    NSTRIP = SLOTS // SW
    PIECES = [[(0, NB)], [(0, 2), (2, 6), (6, NB)]]
    TURNED = [(0, 4), (4, NB - 1)]
    HALF = NT // 2
    ROUTE_FROM = PIECES[1][0][1] + 1
    SKIP = 2.0 * T
    EPS = 1e-5

    ctx = ExitStack()
    with ctx:
        def sb(name, shape, dt=F32):
            return ctx.enter_context(nc.sbuf_tensor(name, shape, dt))

        def sem(name):
            return ctx.enter_context(nc.semaphore(name))

        bank = [ctx.enter_context(nc.psum_tensor(f"bank{i}", [P, 512], F32)) for i in range(8)]

        center = sb("center", [P, P])
        ce = sb("ce", [P, const_early.shape[1]])
        cl = sb("cl", [P, const_late.shape[1]])
        at = [0]

        def part(n):
            at[0] += n
            return ce[:, at[0] - n:at[0]]

        ident, sines = part(P), part(P)
        tri_less_one, rev, iota_place, iota_strip, token_code = part(P), part(E), part(SW), part(NSTRIP), part(NT)
        basis_in, basis_out, basis_turned = cl[:, 0:2 * P], cl[:, 2 * P:3 * P], cl[:, 3 * P:4 * P]
        tri_bf = sb("tri_bf", [P, P], BF16)
        rev_bf = sb("rev_bf", [P, E], BF16)
        token_half = sb("token_half", [P, NT], F16)
        strip_no = sb("strip_no", [P, NSTRIP, NT], I16)
        place_no = sb("place_no", [P, SW, NT], I16)
        warm_in = sb("warm_in", [P, SEQ], BF16)
        ones_bf = sb("ones_bf", [P, P], BF16)
        restart = [[sb(f"restart{n}_{k}", [P, E, (b1 - b0) * TB], BF16) for k, (b0, b1) in enumerate(PIECES[n])]
                   for n in range(2)]
        eps = sb("eps", [P, 1])
        par = sb("par", [P // 2, 1])
        bw = sb("bw", [P, D])
        cwT = sb("cwT", [P, D])
        dsk = sb("dsk", [P, D])
        gate = sb("gate", [P, E])
        gate_c = sb("gate_c", [P, Q])
        w1s = sb("w1s", [P, E, F])
        w2s = sb("w2s", [P, E, FC, D])
        xt = sb("xt", [P, T])
        x1 = sb("x1", [P, NT, D])
        x2 = sb("x2", [P, NT, D])
        xT = sb("xT", [P, 2, SEQ])
        lgT = sb("lgT", [P, 2, SEQ])
        top = sb("top", [P, NT])
        is_top = sb("is_top", [P, NT, E], BF16)
        key = sb("key", [P, NT, E], BF16)
        top_key = sb("top_key", [P, NT])
        chosen = [[sb(f"chosen{n}_{k}", [P, E, (b1 - b0) * TB], BF16) for k, (b0, b1) in enumerate(PIECES[n])]
                  for n in range(2)]
        counted = [[sb(f"counted{n}_{k}", [P, E, (b1 - b0) * TB], BF16) for k, (b0, b1) in enumerate(PIECES[n])]
                   for n in range(2)]
        own_count = sb("own_count", [P, E, NT])
        count = sb("count", [P, NT])
        over = sb("over", [P, NT])
        slot_f = sb("slot_f", [P, NT])
        slot_i = sb("slot_i", [P, NT], I16)
        split_i = sb("split_i", [P, 2, NT], I16)
        hot_place = sb("hot_place", [P, SW, NT], F16)
        hot_strip = sb("hot_strip", [P, NSTRIP, NT], F16)
        hot_tok = sb("hot_tok", [P, NSTRIP, NT], F16)
        unfilled = sb("unfilled", [SW, NSTRIP])
        below = sb("below", [SW, NSTRIP])
        tok_low = sb("tok_low", [SW, NSTRIP])
        tok_high = sb("tok_high", [SW, NSTRIP])
        tok = sb("tok", [P, NS], U32)
        xg = sb("xg", [P, NS, D])
        xc = sb("xc", [P, NS, D])
        xcT = sb("xcT", [P, SLOTS])
        gstat = sb("gstat", [P, NS, 6])
        gmv = sb("gmv", [P, NS, 2])
        gsd = sb("gsd", [P, NS])
        table_load = sb("table_load", [P, 2])
        grs = sb("grs", [P, NS])
        lg = sb("lg", [P, NS, E])
        lgx = sb("lgx", [P, NS])
        pe_ = sb("prob_e", [P, NS, E])
        psm = sb("prob_sum", [P, NS])
        prc = sb("prob_rc", [P, NS])
        gscale = sb("gscale", [P, NS])
        hT = sb("hT", [P, 2, FC, CAP])
        eoT = sb("eoT", [P, SLOTS])
        xnew = sb("xnew", [P, NS, D])
        om = sb("om", [P, 4])
        ct = sb("ct", [P, SEQ + 1])
        st = sb("st", [P, SEQ + 1])
        tmp = sb("tmp", [P, 2, SEQ // 2])
        bt = sb("bt", [P, 2 * P])
        g1 = sb("g1", [P, D + E])
        g2 = sb("g2", [P, D + E])
        gT = sb("gT", [P, 2 * P])
        last_logits = sb("last_logits", [P, TB, E])
        sstat = sb("sstat", [P, 2, TB, 6])
        smv = sb("smv", [P, 2, TB, 2])
        ssd = sb("ssd", [P, 2, TB])
        srs = sb("srs", [P, 2, TB])
        snb = sb("snb", [P, 2, TB])
        u = sb("u", [P, 2, TB, D])
        ud = sb("ud", [P, TB, D])
        w = sb("w", [P, 2, TB, D])
        uT = sb("uT", [P, 2, SEQ])
        vq = sb("vq", [P, SEQ])
        va = sb("va", [P, SEQ])
        vb = sb("vb", [P, SEQ])
        z = sb("z", [P, SEQ])
        zc = sb("zc", [P, 2, SEQ])
        zs = sb("zs", [P, 2, SEQ])

        x1_dram = nc.dram_tensor("x1_scratch", [T, D], F32, kind="Internal").ap()
        x_rows = x_in.rearrange("b s d -> (b s) d")
        out_rows = out.rearrange("b s d -> (b s) d")

        def tiles(rows, b):
            return rows[b * SEQ:(b + 1) * SEQ, :].rearrange("(c p) d -> p c d", p=P)

        warm_set, eps_set, place_set, d_center = sem("warm_set"), sem("eps_set"), sem("place_set"), sem("d_center")
        d_early, d_late, d_gate, d_par, d_bw, d_cw, d_dsk = (sem(f"d_{n}") for n in
                                                             ("early", "late", "gate", "par", "bw", "cw", "dsk"))
        d_w1 = [sem(f"d_w1_{i}") for i in range(2)]
        d_w2 = [sem(f"d_w2_{i}") for i in range(2)]
        d_xt = [sem(f"d_xt{b}") for b in range(NB)]
        d_x1 = [sem(f"d_x1_{b}") for b in range(NB)]
        d_fill = sem("d_fill")
        d_gather = [sem(f"d_gather{j}") for j in range(NS)]
        d_scatter = sem("d_scatter")
        d_out = sem("d_out")
        pool_set, pool_chain, dve_chain = sem("pool_set"), sem("pool_chain"), sem("dve_chain")
        set_ps = sem("set_ps")
        gate_ps, gate_sb, omega_ps, tables = sem("gate_ps"), sem("gate_sb"), sem("omega_ps"), sem("tables")
        xT_ps, xT_sb, logits = sem("xT_ps"), sem("xT_sb"), sem("logits")
        lgT_ps, lgT_sb = sem("lgT_ps"), sem("lgT_sb")

        def piece(n, k):
            return n * len(PIECES[0]) + k

        PITCH = D + E

        def last_y(c):
            b, at_ = (bank[4], c * PITCH) if c < TB - 1 else (bank[5], 0)
            return b[:, at_:at_ + PITCH]

        def hot_parts(n, k):
            t0, t1 = (b * TB for b in PIECES[n][k])
            return [(t0, (t0 + t1) // 2), ((t0 + t1) // 2, t1)] if n == 0 else [(t0, t1)]

        def parts_before(n, k):
            return sum(len(hot_parts(m, j)) for m in range(2) for j in range(len(PIECES[m])) if (m, j) < (n, k))

        marked, ranked, rank_read, hot, placed, indexed = (sem(n) for n in ("marked", "ranked", "rank_read", "hot",
                                                                            "placed", "indexed"))
        centered, slotT_ps, slotT_sb, slot_logits = (sem(n) for n in ("centered", "slotT_ps", "slotT_sb", "slot_logits"))
        gsd_r, lg_r, pe_r = (sem(n) for n in ("gsd_r", "lg_r", "pe_r"))
        h_ps, h_sb, eo_ps, eo_sb, row_ps, row_sb = (sem(n) for n in ("h_ps", "h_sb", "eo_ps", "eo_sb", "row_ps",
                                                                     "row_sb"))
        svar, ssd_r, snb_r, u_r, ud_r, w_r = (sem(n) for n in ("svar", "ssd_r", "snb_r", "u_r", "ud_r", "w_r"))
        wT_ps, wT_sb = sem("wT_ps"), sem("wT_sb")
        uT_ps, uT_sb, v_ps, vq_sb, va_r, vb_r, z_r = (sem(n) for n in ("uT_ps", "uT_sb", "v_ps", "vq_sb", "va_r",
                                                                       "vb_r", "z_r"))
        zc_r, zs_r, y_ps, x2_r = (sem(n) for n in ("zc_r", "zs_r", "y_ps", "x2_r"))

        def experts_before(j):
            return -(-(j + 1) * P // CAP)

        def tiles_before(e):
            return -(-(e + 1) * CAP // P)

        def steps(text):
            return [(word[0], int(word[1])) for word in text.split()]

        pe_steps = steps("i0 x1 i1 x2 u0 i2 d0 i3 u1 i4 l0 l1 u2 i5 d1 i6 i7 l2 l3 l4 l5 u3 i8 i9 d2 l6 l7 l8 l9 "
                         "u4 o0 o1 d3 u5 o2 o3 d4 o4 u6 o5 d5 u7 o6 d6 o7 d7 o8 o9")
        dve_steps = steps("i0 i1 i2 i3 i4 d0 i5 i6 i7 i8 d1 i9 d2 l0 f0 o0 o1 d3 p7 "
                          "o2 o3 d4 p8 o4 o5 d5 o6 d6 o7 d7 o8 o9")
        act_steps = steps("i0 i1 u0 i2 i3 u1 i4 u2 i5 i6 i7 u3 i8 i9 g0 e0 u4 u5 u6 u7")

        block = ctx.enter_context(nc.Block())

        @block.sync
        def _(sp):
            sp.dma_start(center[:, :], const_center).then_inc(d_center, 16)
            for b in range(NB):
                sp.dma_start(xt[:, b * SEQ:(b + 1) * SEQ], x_turned[:, b * SEQ:(b + 1) * SEQ]).then_inc(d_xt[b], 16)
            sp.dma_start(bw[:, :], b_w).then_inc(d_bw, 16)
            sp.dma_start(cwT[:, :], c_w_turned).then_inc(d_cw, 16)
            sp.dma_start(cl[:, :], const_late).then_inc(d_late, 16)
            for i in range(2):
                h = slice(i * E // 2, (i + 1) * E // 2)
                sp.dma_start(w1s[:, h, :], w1[h].rearrange("e d f -> d e f")).then_inc(d_w1[i], 16)
                for e in range(i * E // 2, (i + 1) * E // 2):
                    sp.dma_start(w2s[:, e, :, :], w2[e].rearrange("(c p) d -> p c d", p=P)).then_inc(d_w2[i], 16)
            sp.dma_start(dsk[:, :], d_skip.partition_broadcast(P)).then_inc(d_dsk, 16)
            sp.wait_ge(d_gather[NS - 1], 16)
            sp.dma_start(x1_dram, x_rows).then_inc(d_fill, 16)
            sp.wait_ge(d_fill, 16)
            sp.wait_ge(d_scatter, 16 * NS)
            for b in range(NB):
                sp.dma_start(x1[:, b * TB:(b + 1) * TB, :], tiles(x1_dram, b)).then_inc(d_x1[b], 16)
            for b in range(NB):
                sp.wait_ge(x2_r, b + 1)
                sp.dma_start(tiles(out_rows, b), x2[:, b * TB:(b + 1) * TB, :]).then_inc(d_out, 16)
            sp.wait_ge(d_out, 16 * NB)
            sp.wait_ge(d_scatter, 16 * NS * 2)

        @block.gpsimd
        def _(pool):
            links = [0]

            def link(ins):
                links[0] += 1
                ins.then_inc(pool_chain, 1)
                pool.wait_ge(pool_chain, links[0])

            nc.gpsimd.memset(eps[:, :], EPS).then_inc(eps_set, 1)
            for n in range(2):
                for mask in restart[n]:
                    link(nc.gpsimd.memset(mask[:, :, :], 1.0))
                    nc.gpsimd.memset(mask[:, :, 0:1], 0.0)
            pool.wait_ge(d_early, 16)
            nc.gpsimd.tensor_copy(rev_bf[:, :], rev)
            nc.gpsimd.tensor_copy(tri_bf[:, :], tri_less_one).then_inc(pool_set, 1)
            nc.gpsimd.tensor_copy(strip_no[:, :, :], iota_strip.unsqueeze(2).broadcast_to([P, NSTRIP, NT]))
            nc.gpsimd.tensor_copy(token_half[:, :], token_code).then_inc(pool_set, 1)
            nc.gpsimd.memset(xg[:, :, :], 0.0).then_inc(pool_set, 1)

            def gather(n):
                pool.wait_ge(indexed, n + 1)
                pool.wait_ge(pool_set, 3)
                if n == 1:
                    pool.wait_ge(d_out, 16 * NB)
                    pool.wait_ge(row_sb, NS)
                for j in range(NS):
                    pool.indirect_dma_start(xg[:, j, :], None, (x_rows, out_rows)[n],
                                            bass.IndirectOffsetOnAxis(ap=tok[:, j:j + 1], axis=0),
                                            bounds_check=T - 1, oob_is_err=False).then_inc(d_gather[j], 16)

            def scatter(n):
                if n == 0:
                    pool.wait_ge(d_fill, 16)
                for j in range(NS):
                    pool.wait_ge(row_sb, n * NS + j + 1)
                    pool.indirect_dma_start((x1_dram, out_rows)[n],
                                            bass.IndirectOffsetOnAxis(ap=tok[:, j:j + 1], axis=0),
                                            xnew[:, j, :], None,
                                            bounds_check=T - 1, oob_is_err=False).then_inc(d_scatter, 16)

            gather(0)
            scatter(0)
            pool.wait_ge(d_dsk, 16)
            pool.wait_ge(tables, 1)

            def skip_product(b):
                pool.wait_ge(u_r, b + 1)
                if b >= 1:
                    pool.wait_ge(w_r, b)
                nc.gpsimd.tensor_tensor(ud[:, :, :], u[:, b % 2, :, :],
                                        dsk[:, :].unsqueeze(1).broadcast_to([P, TB, D]), ALU.mult).then_inc(ud_r, 1)

            def skip_sum(b):
                pool.wait_ge(ud_r, b + 1)
                if b >= 2:
                    pool.wait_ge(x2_r, b - 1)
                nc.gpsimd.tensor_tensor(w[:, b % 2, :, :], ud[:, :, :], x1[:, b * TB:(b + 1) * TB, :],
                                        ALU.add).then_inc(w_r, 1)

            def turn_back(b):
                pool.wait_ge(vq_sb, b + 1)
                if b >= 1:
                    pool.wait_ge(z_r, b)
                nc.gpsimd.tensor_tensor(vb[:, :], vq[:, :], st[:, 0:SEQ], ALU.mult).then_inc(vb_r, 1)

            def turn_forth(b):
                pool.wait_ge(z_r, b + 1)
                if b >= 2:
                    pool.wait_ge(y_ps, b - 1)
                nc.gpsimd.tensor_tensor(zs[:, b % 2, :], z[:, :], st[:, 0:SEQ], ALU.mult).then_inc(zs_r, 1)

            for i in range(-1, NB):
                if i >= 0:
                    turn_back(i)
                if i + 1 < NB:
                    skip_product(i + 1)
                if i >= 0:
                    turn_forth(i)
                if i + 1 < NB:
                    skip_sum(i + 1)
            gather(1)
            scatter(1)

        @block.scalar
        def _(act):
            act.dma_start(gate[:, :], gate_w).then_inc(d_gate, 16)
            act.dma_start(ce[:, :], const_early).then_inc(d_early, 16)
            act.dma_start(par[:, :], a_params.rearrange("(n o) -> n o", o=1)).then_inc(d_par, 16)
            act.wait_ge(eps_set, 1)
            nc.scalar.activation(table_load[:, 0:1], eps[:, 0:1], ACT.Sqrt)
            act.wait_ge(d_early, 16)
            nc.scalar.copy(place_no[:, :, :], iota_place.unsqueeze(2).broadcast_to([P, SW, NT])).then_inc(place_set, 1)
            for k, (b0, b1) in enumerate(TURNED):
                rows = (b1 - b0) * Q
                act.wait_ge(lgT_ps, k + 1)
                nc.scalar.copy(lgT[0:rows, k, :], bank[2 + k][0:rows, :]).then_inc(lgT_sb, 1)
            act.wait_ge(set_ps, 1)
            nc.scalar.copy(g1[:, 0:D], bank[4][:, 0:P])
            nc.scalar.copy(g2[:, 0:D], bank[4][:, P:2 * P])
            nc.scalar.copy(bt[:, :], bank[6][:, 0:2 * P]).then_inc(tables, 1)
            act.wait_ge(set_ps, 2)
            nc.scalar.copy(gT[:, :], bank[4][:, 0:2 * P]).then_inc(tables, 1)
            act.wait_ge(set_ps, 3)
            nc.scalar.copy(g1[:, D:D + E], bank[4][:, 0:E])
            nc.scalar.copy(g2[:, D:D + E], bank[4][:, E:2 * E]).then_inc(tables, 1)

            def copy_xT(b):
                act.wait_ge(xT_ps, b + 1)
                if b >= 2:
                    act.wait_ge(logits, len(TURNED) + 1 + b - 1)
                nc.scalar.copy(xT[:, b % 2, :], bank[1][:, :]).then_inc(xT_sb, 1)

            def slots(n):
                def slot_in(j):
                    act.wait_ge(slotT_ps, n * NS + j + 1)
                    nc.scalar.copy(xcT[:, j * P:(j + 1) * P],
                                   bank[j % 2][:, 0:P]).then_inc(slotT_sb, 1)

                def relu(e):
                    for half in range(2):
                        act.wait_ge(h_ps, n * 2 * E + 2 * e + half + 1)
                        if e >= 2:
                            act.wait_ge(eo_ps, n * E + e - 1)
                        nc.scalar.activation(hT[:, e % 2, half * HC:(half + 1) * HC, :],
                                             bank[4 + half][:, 0:HC * CAP]
                                             .rearrange("p (c s) -> p c s", c=HC), ACT.Relu).then_inc(h_sb, 1)

                for kind, i in act_steps:
                    if kind == "i":
                        slot_in(i)
                    elif kind == "g":
                        act.wait_ge(centered, n * NS + NS)
                        nc.scalar.activation(gsd[:, :], gmv[:, :, 1], ACT.Sqrt, bias=eps[:, 0:1]).then_inc(gsd_r, 1)
                        nc.scalar.activation(table_load[:, 1:2], eps[:, 0:1], ACT.Exp)
                    elif kind == "e":
                        act.wait_ge(lg_r, n + 1)
                        nc.scalar.activation(pe_[:, :, :], lg[:, :, :], ACT.Exp).then_inc(pe_r, 1)
                    else:
                        relu(i)

            slots(0)

            def deviation(b):
                act.wait_ge(svar, b + 1)
                if b >= 2:
                    act.wait_ge(snb_r, b - 1)
                nc.scalar.activation(ssd[:, b % 2, :], smv[:, b % 2, :, 1], ACT.Sqrt, bias=eps[:, 0:1]).then_inc(ssd_r, 1)

            def normalise(b):
                act.wait_ge(snb_r, b + 1)
                if b >= 2:
                    act.wait_ge(ud_r, b - 1)
                    act.wait_ge(uT_ps, b - 1)
                for c in range(TB):
                    ins = nc.scalar.activation(u[:, b % 2, c, :], x1[:, b * TB + c, :], ACT.Identity,
                                               bias=snb[:, b % 2, c:c + 1], scale=srs[:, b % 2, c:c + 1])
                ins.then_inc(u_r, 1)

            for i in range(-2, NB + 2):
                if 0 <= i < NB:
                    act.wait_ge(v_ps, i + 1)
                    if i >= 1:
                        act.wait_ge(vb_r, i)
                    nc.scalar.copy(vq[:, :], bank[5][:, :]).then_inc(vq_sb, 1)
                if i + 2 < NB:
                    deviation(i + 2)
                if 0 <= i + 1 < NB:
                    act.wait_ge(uT_ps, i + 2)
                    if i >= 1:
                        act.wait_ge(v_ps, i)
                    nc.scalar.copy(uT[:, (i + 1) % 2, :], bank[0][:, :]).then_inc(uT_sb, 1)
                if i + 2 < NB:
                    normalise(i + 2)
                if i == NB - 1:
                    act.wait_ge(wT_ps, 1)
                    act.wait_ge(v_ps, NB - 1)
                    nc.scalar.copy(uT[:, NB % 2, :], bank[0][:, :]).then_inc(wT_sb, 1)
                if 0 <= i - 1 < NB - 1:
                    copy_xT(i - 1)
            slots(1)

        @block.vector
        def _(dve):
            links = [0]

            def link(ins):
                links[0] += 1
                ins.then_inc(dve_chain, 1)
                dve.wait_ge(dve_chain, links[0])

            V = nc.vector
            V.memset(ones_bf[:, :], 1.0)
            V.memset(warm_in[:, :], 1.0).then_inc(warm_set, 1)
            link(V.memset(gate_c[:, :], 0.0))
            dve.wait_ge(gate_ps, 1)
            V.tensor_copy(gate_c[:, 0:E], bank[5][:, 0:E]).then_inc(gate_sb, 1)

            def eigenvalues():
                dve.wait_ge(omega_ps, 1)
                link(V.tensor_copy(om[:, 0:1], bank[5][:, E:E + 1]))
                link(V.tensor_tensor(om[:, 1:2], om[:, 0:1], om[:, 0:1], ALU.mult))
                link(V.tensor_scalar(om[:, 2:3], om[:, 1:2], 1.0, None, ALU.add))
                link(V.reciprocal(om[:, 3:4], om[:, 2:3]))
                link(V.tensor_scalar(om[:, 2:3], om[:, 1:2], -1.0, 1.0, ALU.mult, ALU.add))
                V.memset(ct[:, 0:1], 1.0)
                V.memset(st[:, 0:1], 0.0)
                V.tensor_tensor(ct[:, 1:2], om[:, 2:3], om[:, 3:4], ALU.mult)
                link(V.scalar_tensor_tensor(st[:, 1:2], om[:, 0:1], -2.0, om[:, 3:4], ALU.mult, ALU.mult))

            def powers(first, last):
                for level in range(first, last):
                    m = 1 << level
                    V.tensor_scalar(tmp[:, 0, 0:m], st[:, 1:m + 1], st[:, m:m + 1], None, ALU.mult)
                    link(V.tensor_scalar(tmp[:, 1, 0:m], ct[:, 1:m + 1], st[:, m:m + 1], None, ALU.mult))
                    V.scalar_tensor_tensor(ct[:, m + 1:2 * m + 1], ct[:, 1:m + 1], ct[:, m:m + 1], tmp[:, 0, 0:m],
                                           ALU.mult, ALU.subtract)
                    link(V.scalar_tensor_tensor(st[:, m + 1:2 * m + 1], st[:, 1:m + 1], ct[:, m:m + 1],
                                                tmp[:, 1, 0:m], ALU.mult, ALU.add))

            def rate(logits_in, t0, wd):
                ts = slice(t0, t0 + wd)

                def by_batch(a):
                    return a.rearrange("p (b c) e -> p b c e", c=TB)

                link(V.reduce_max(top[:, ts].rearrange("p (b c) -> p b c", c=TB), logits_in, axis=AX))
                return V.tensor_tensor(by_batch(is_top[:, ts, :]), logits_in,
                                       by_batch(top[:, ts].unsqueeze(2).broadcast_to([P, wd, E])), ALU.is_equal)

            def choose(n, k, t0, wd):
                first = PIECES[n][k][0] * TB
                ts = slice(t0, t0 + wd)
                link(V.tensor_tensor(key[:, ts, :], is_top[:, ts, :],
                                     rev_bf[:, :].unsqueeze(1).broadcast_to([P, wd, E]), ALU.mult))
                link(V.reduce_max(top_key[:, ts], key[:, ts, :], axis=AX))
                return V.tensor_tensor(chosen[n][k][:, :, t0 - first:t0 - first + wd].rearrange("p e t -> p t e"),
                                       key[:, ts, :], top_key[:, ts].unsqueeze(2).broadcast_to([P, wd, E]), ALU.is_equal)

            def plain(a, wd):
                return a[:, 0:wd * E].rearrange("p (b c e) -> p b c e", c=TB, e=E)

            def mark(n, k, parts=(True, True)):
                b0, b1 = PIECES[n][k]
                if n == 0:
                    for g, (g0, g1_) in enumerate(TURNED):
                        dve.wait_ge(logits, g + 1)
                        nb = g1_ - g0
                        turned = bank[2 + g][:, 0:TB * nb * Q].rearrange("p (c b q) -> p b c q", b=nb, q=Q)
                        ins = rate(turned[:, :, :, 0:E], g0 * TB, nb * TB)
                        if g == 0:
                            link(ins)
                            choose(n, k, g0 * TB, nb * TB)
                            powers(0, 1)
                    dve.wait_ge(logits, len(TURNED) + 1)
                    link(rate(plain(bank[1], TB), (NB - 1) * TB, TB))
                    t0 = TURNED[-1][0] * TB
                    link(choose(n, k, t0, NT - t0))
                else:
                    wd = (b1 - b0) * TB
                    dve.wait_ge(logits, len(TURNED) + 1 + b1)
                    if parts[0]:
                        link(rate(plain(bank[2 + k % 2], wd), b0 * TB, wd))
                    if not parts[1]:
                        return
                    link(choose(n, k, b0 * TB, wd))
                count_up(n, k)

            def count_up(n, k):
                V.tensor_tensor_scan(counted[n][k][:, :, :].rearrange("p e t -> p (e t)"),
                                     restart[n][k][:, :, :].rearrange("p e t -> p (e t)"),
                                     chosen[n][k][:, :, :].rearrange("p e t -> p (e t)"), 0.0,
                                     ALU.mult, ALU.add).then_inc(marked, 1)

            def make_hot(n, k, parts=(True, True)):
                b0, b1 = PIECES[n][k]
                wd = (b1 - b0) * TB
                ts = slice(b0 * TB, b1 * TB)
                if parts[0]:
                    dve.wait_ge(ranked, piece(n, k) + 1)
                    if n == 0:
                        dve.wait_ge(pool_set, 2)
                        dve.wait_ge(place_set, 1)
                    rank = bank[2 + k % 2][:, 0:wd * E].rearrange("p (e t) -> p e t", e=E)
                    V.tensor_tensor(own_count[:, :, ts], rank, chosen[n][k][:, :, :], ALU.mult).then_inc(rank_read, 1)
                    dve.wait_ge(rank_read, piece(n, k) + 1)
                    link(V.reduce_sum(count[:, ts], own_count[:, :, ts].rearrange("p e t -> p t e"), axis=AX))
                    V.tensor_scalar(over[:, ts], count[:, ts], CAP + 0.5, SKIP, ALU.is_gt, ALU.mult)
                    link(V.scalar_tensor_tensor(slot_f[:, ts], top_key[:, ts], -float(CAP), count[:, ts],
                                                ALU.mult, ALU.add))
                    link(V.scalar_tensor_tensor(slot_i[:, ts], slot_f[:, ts], float(SLOTS - 1), over[:, ts],
                                                ALU.add, ALU.add))
                    V.tensor_scalar(split_i[:, 0, ts], slot_i[:, ts], SW - 1, None, ALU.bitwise_and)
                    link(V.tensor_scalar(split_i[:, 1, ts], slot_i[:, ts], SW.bit_length() - 1, None,
                                         ALU.logical_shift_right))
                if not parts[1]:
                    return
                link(V.tensor_tensor(hot_strip[:, :, ts], split_i[:, 1, ts].unsqueeze(1).broadcast_to([P, NSTRIP, wd]),
                                     strip_no[:, :, ts], ALU.is_equal))
                V.tensor_tensor(hot_tok[:, :, ts], hot_strip[:, :, ts],
                                token_half[:, ts].unsqueeze(1).broadcast_to([P, NSTRIP, wd]), ALU.mult)
                for t0, t1 in hot_parts(n, k):
                    V.tensor_tensor(hot_place[:, :, t0:t1],
                                    split_i[:, 0, t0:t1].unsqueeze(1).broadcast_to([P, SW, t1 - t0]),
                                    place_no[:, :, t0:t1], ALU.is_equal).then_inc(hot, 1)

            def index(n):
                code = bank[7][0:SW, 0:NSTRIP]
                dve.wait_ge(placed, n + 1)
                V.tensor_scalar(unfilled[:, :], code, 0.0, SKIP / (HALF * P), ALU.is_equal, ALU.mult)
                link(V.tensor_scalar(below[:, :], code, -1.0, -1.0, ALU.mult, ALU.add))
                V.scalar_tensor_tensor(tok_low[:, :], code, -1.0, below[:, :], ALU.add, ALU.max)
                link(V.scalar_tensor_tensor(tok_high[:, :], code, 0.0, unfilled[:, :], ALU.is_lt, ALU.add))
                if n == 1:
                    dve.wait_ge(d_scatter, 16 * NS)
                for r in range(P // SW):
                    ins = V.scalar_tensor_tensor(tok[r * SW:(r + 1) * SW, :], tok_high[:, r::P // SW], float(HALF * P),
                                                 tok_low[:, r::P // SW], ALU.mult, ALU.add)
                ins.then_inc(indexed, 1)

            def slots(n):
                def slot_in(j):
                    dve.wait_ge(d_gather[j], 16 * (n + 1))
                    link(V.bn_stats(gstat[:, j, :], xg[:, j, :]))
                    link(V.bn_aggr(gmv[:, j, :], gstat[:, j, :]))
                    ins = V.tensor_scalar(xc[:, j, :], xg[:, j, :], gmv[:, j, 0:1], None, ALU.subtract)
                    ins.then_inc(centered, 1)

                def half_prob():
                    dve.wait_ge(gsd_r, n + 1)
                    link(V.reciprocal(grs[:, :], gsd[:, :]))
                    dve.wait_ge(slot_logits, n + 1)
                    link(V.tensor_tensor(lg[:, :, :], bank[2][:, 0:NS * E].rearrange("p (t e) -> p t e", e=E),
                                         grs[:, :].unsqueeze(2).broadcast_to([P, NS, E]), ALU.mult))
                    link(V.reduce_max(lgx[:, :], lg[:, :, :], axis=AX))
                    V.tensor_tensor(lg[:, :, :], lg[:, :, :], lgx[:, :].unsqueeze(2).broadcast_to([P, NS, E]),
                                    ALU.subtract).then_inc(lg_r, 1)

                def half_prob_end():
                    dve.wait_ge(pe_r, n + 1)
                    link(V.reduce_sum(psm[:, :], pe_[:, :, :], axis=AX))
                    link(V.reciprocal(prc[:, :], psm[:, :]))
                    link(V.scalar_tensor_tensor(gscale[:, :], grs[:, :], 0.5, prc[:, :], ALU.mult, ALU.mult))

                for kind, i in dve_steps:
                    if kind == "i":
                        slot_in(i)
                    elif kind == "l":
                        half_prob()
                    elif kind == "d":
                        dve.wait_ge(eo_ps, n * E + i + 1)
                        V.tensor_copy(eoT[:, i * CAP:(i + 1) * CAP], bank[6 + i % 2][:, 0:CAP]).then_inc(eo_sb, 1)
                    elif kind == "f":
                        half_prob_end()
                    elif kind == "p":
                        if n == 0:
                            powers(i, i + 1)
                    else:
                        dve.wait_ge(row_ps, n * NS + i + 1)
                        V.scalar_tensor_tensor(xnew[:, i, :], bank[2 + i % 2][:, 0:P],
                                               gscale[:, i:i + 1], xg[:, i, :], ALU.mult, ALU.add).then_inc(row_sb, 1)

            eigenvalues()
            dve.wait_ge(pool_set, 1)
            for k in range(len(PIECES[0])):
                mark(0, k)
                powers(1, 2)
                make_hot(0, k)
            powers(2, 3)
            index(0)
            powers(3, 7)
            slots(0)

            def stats(b):
                dve.wait_ge(d_x1[b], 16)
                for c in range(TB):
                    ins = V.bn_stats(sstat[:, b % 2, c, :], x1[:, b * TB + c, :])
                link(ins)
                if b >= 2:
                    dve.wait_ge(ssd_r, b - 1)
                for c in range(TB):
                    ins = V.bn_aggr(smv[:, b % 2, c, :], sstat[:, b % 2, c, :])
                ins.then_inc(svar, 1)

            def shift(b):
                dve.wait_ge(svar, b + 1)
                dve.wait_ge(ssd_r, b + 1)
                if b >= 2:
                    dve.wait_ge(u_r, b - 1)
                link(V.reciprocal(srs[:, b % 2, :], ssd[:, b % 2, :]))
                V.scalar_tensor_tensor(snb[:, b % 2, :], smv[:, b % 2, :, 0], -1.0, srs[:, b % 2, :],
                                       ALU.mult, ALU.mult).then_inc(snb_r, 1)

            def add_back(b):
                dve.wait_ge(y_ps, b + 1)
                dve.wait_ge(w_r, b + 1)
                V.tensor_tensor(x2[:, b * TB:(b + 1) * TB, :], bank[6][:, :].rearrange("p (c d) -> p c d", c=TB),
                                w[:, b % 2, :, :], ALU.add).then_inc(x2_r, 1)

            def finish_last():
                y3 = bank[4][:, 0:(TB - 1) * PITCH].rearrange("p (c d) -> p c d", c=TB - 1)
                t0 = (NB - 1) * TB
                V.tensor_tensor(x2[:, t0:t0 + TB - 1, :], y3[:, :, 0:D], w[:, (NB - 1) % 2, 0:TB - 1, :], ALU.add)
                V.tensor_tensor(x2[:, t0 + TB - 1, :], bank[5][:, 0:D], w[:, (NB - 1) % 2, TB - 1, :],
                                ALU.add).then_inc(x2_r, 1)

            def mark_last():
                b0, b1 = PIECES[1][-1]
                wd = (b1 - b0 - 1) * TB
                in_bank = plain(bank[2], wd + TB)
                dve.wait_ge(logits, len(TURNED) + 1 + NB)
                rate(in_bank[:, 0:b1 - b0 - 1], b0 * TB, wd)
                link(V.tensor_copy(last_logits[:, :, :], bank[2][:, wd * E:(wd + TB) * E]
                                   .rearrange("p (c e) -> p c e", c=TB)))
                dve.wait_ge(y_ps, NB)
                dve.wait_ge(w_r, NB)
                y3 = bank[4][:, 0:(TB - 1) * PITCH].rearrange("p (c d) -> p c d", c=TB - 1)
                V.tensor_tensor(last_logits[:, 0:TB - 1, :], y3[:, :, D:PITCH],
                                last_logits[:, 0:TB - 1, :], ALU.add)
                link(V.tensor_tensor(last_logits[:, TB - 1, :], bank[5][:, D:PITCH],
                                     last_logits[:, TB - 1, :], ALU.add))
                link(rate(last_logits[:, :, :].unsqueeze(1), (NB - 1) * TB, TB))
                link(choose(1, len(PIECES[1]) - 1, b0 * TB, wd + TB))
                count_up(1, len(PIECES[1]) - 1)

            for i in range(-2, NB):
                if i + 2 < NB:
                    stats(i + 2)
                if 0 <= i < NB:
                    dve.wait_ge(v_ps, i + 1)
                    V.tensor_tensor(va[:, :], bank[4][:, :], ct[:, 0:SEQ], ALU.mult).then_inc(va_r, 1)
                if i == NB - 1:
                    mark(1, 1)
                if i >= 1:
                    add_back(i - 1)
                if i + 2 < NB:
                    shift(i + 2)
                if 0 <= i < NB:
                    dve.wait_ge(va_r, i + 1)
                    dve.wait_ge(vb_r, i + 1)
                    if i >= 1:
                        dve.wait_ge(zs_r, i)
                    V.tensor_tensor_scan(z[:, :], va[:, :], vb[:, :], 0.0, ALU.add, ALU.add).then_inc(z_r, 1)
                    dve.wait_ge(z_r, i + 1)
                    if i >= 2:
                        dve.wait_ge(y_ps, i - 1)
                    V.tensor_tensor(zc[:, i % 2, :], z[:, :], ct[:, 0:SEQ], ALU.mult).then_inc(zc_r, 1)
                if i == ROUTE_FROM:
                    mark(1, 0, (True, False))
                if i == ROUTE_FROM + 1:
                    mark(1, 0, (False, True))
                if i == ROUTE_FROM + 2:
                    make_hot(1, 0, (True, False))
                if i == ROUTE_FROM + 3:
                    make_hot(1, 0, (False, True))
            make_hot(1, 1)
            mark_last()
            finish_last()
            make_hot(1, 2)
            index(1)
            slots(1)

        @block.tensor
        def _(pe):
            M = nc.tensor.matmul

            def keep_warm(n, to=4):
                for _ in range(n):
                    M(bank[to][:, :], ones_bf[:, :], warm_in[:, :], start=True, stop=True)

            pe.wait_ge(warm_set, 1)
            keep_warm(6)
            pe.wait_ge(d_center, 16)
            pe.wait_ge(d_gate, 16)
            M(bank[5][:, 0:E], center[:, :], gate[:, :], start=True, stop=True).then_inc(gate_ps, 1)
            keep_warm(2)
            pe.wait_ge(gate_sb, 1)

            def omega():
                pe.wait_ge(d_early, 16)
                pe.wait_ge(d_par, 16)
                M(bank[5][:, E:E + 1], sines[0:P // 2, :], par[:, :], start=True, stop=True).then_inc(omega_ps, 1)

            def turn_x2(b):
                pe.wait_ge(x2_r, b + 1)
                if b >= 1:
                    pe.wait_ge(xT_sb, b)
                for c in range(TB):
                    ins = nc.tensor.transpose(bank[1][:, c * P:(c + 1) * P], x2[:, b * TB + c, :], ident)
                ins.then_inc(xT_ps, 1)

            def gate_turned(k):
                for j, b in enumerate(range(*TURNED[k])):
                    pe.wait_ge(d_xt[b], 16)
                    ins = M(bank[2 + k][j * Q:(j + 1) * Q, :], gate_c[:, :], xt[:, b * SEQ:(b + 1) * SEQ],
                            start=True, stop=True)
                    if b + 1 < TURNED[k][1]:
                        keep_warm(2)
                ins.then_inc(lgT_ps, 1)

            def turn_logits(k):
                rows = (TURNED[k][1] - TURNED[k][0]) * Q
                pe.wait_ge(lgT_sb, k + 1)
                for c in range(TB):
                    ins = nc.tensor.transpose(bank[2 + k][:, c * rows:(c + 1) * rows],
                                              lgT[0:rows, k, c * P:(c + 1) * P], ident[0:rows, 0:rows])
                ins.then_inc(logits, 1)

            def gate_last():
                pe.wait_ge(d_xt[NB - 1], 16)
                for c in range(TB):
                    t = (NB - 1) * TB + c
                    ins = M(bank[1][:, c * E:(c + 1) * E], xt[:, t * P:(t + 1) * P], gate_c[:, 0:E],
                            start=True, stop=True)
                ins.then_inc(logits, 1)

            def gate_x2(b):
                k = [b0 <= b < b1 for b0, b1 in PIECES[1]].index(True)
                pe.wait_ge(xT_sb, b + 1)
                if k >= 2 and b == PIECES[1][k][0]:
                    pe.wait_ge(rank_read, piece(1, k - 2) + 1)
                for c in range(TB):
                    t = (b - PIECES[1][k][0]) * TB + c
                    ins = M(bank[2 + k % 2][:, t * E:(t + 1) * E], xT[:, b % 2, c * P:(c + 1) * P], gate_c[:, 0:E],
                            start=True, stop=True)
                ins.then_inc(logits, 1)

            def rank(n, k):
                wd = (PIECES[n][k][1] - PIECES[n][k][0]) * TB
                pe.wait_ge(marked, piece(n, k) + 1)
                q = bank[2 + k % 2][:, 0:wd * E].rearrange("p (e t) -> p e t", e=E)
                for before in range(k):
                    last = (PIECES[n][before][1] - PIECES[n][before][0]) * TB - 1
                    M(q, ones_bf[:, :], counted[n][before][:, :, last:last + 1].broadcast_to([P, E, wd]),
                      start=(before == 0), stop=False)
                M(q, ones_bf[:, :], counted[n][k][:, :, :], start=(k == 0), stop=False)
                M(q, tri_bf[:, :], chosen[n][k][:, :, :], start=False, stop=True).then_inc(ranked, 1)

            def place(n, k):
                for part_no, (t0, t1) in enumerate(hot_parts(n, k)):
                    pe.wait_ge(hot, parts_before(n, k) + part_no + 1)
                    for t in range(t0, t1):
                        ins = M(bank[7][0:SW, 0:NSTRIP], hot_place[:, :, t], hot_tok[:, :, t],
                                start=(t == 0), stop=(t == NT - 1))
                if k == len(PIECES[n]) - 1:
                    ins.then_inc(placed, 1)

            def slots(n):
                for kind, i in pe_steps:
                    if kind == "x":
                        keep_warm(i)
                    elif kind == "i":
                        pe.wait_ge(centered, n * NS + i + 1)
                        if i >= 2:
                            pe.wait_ge(slotT_sb, n * NS + i - 1)
                        nc.tensor.transpose(bank[i % 2][:, 0:P], xc[:, i, :], ident)\
                            .then_inc(slotT_ps, 1)
                    elif kind == "l":
                        pe.wait_ge(slotT_sb, n * NS + i + 1)
                        pe.wait_ge(indexed, n + 1)
                        ins = M(bank[2][:, i * E:(i + 1) * E], xcT[:, i * P:(i + 1) * P], gate[:, :],
                                start=True, stop=True)
                        if i == NS - 1:
                            ins.then_inc(slot_logits, 1)
                    elif kind == "u":
                        if n == 0 and i % (E // 2) == 0:
                            pe.wait_ge(d_w1[i // (E // 2)], 16)
                        pe.wait_ge(slotT_sb, n * NS + tiles_before(i))
                        for half in range(2):
                            if i >= 1:
                                pe.wait_ge(h_sb, n * 2 * E + 2 * (i - 1) + half + 1)
                            for c in range(HC):
                                ch = half * HC + c
                                ins = M(bank[4 + half][:, c * CAP:(c + 1) * CAP],
                                        w1s[:, i, ch * P:(ch + 1) * P], xcT[:, i * CAP:(i + 1) * CAP],
                                        start=True, stop=True)
                            ins.then_inc(h_ps, 1)
                    elif kind == "d":
                        if n == 0 and i % (E // 2) == 0:
                            pe.wait_ge(d_w2[i // (E // 2)], 16 * (E // 2))
                        pe.wait_ge(h_sb, n * 2 * E + 2 * i + 2)
                        if i >= 2:
                            pe.wait_ge(eo_sb, n * E + i - 1)
                        for c in range(FC):
                            ins = M(bank[6 + i % 2][:, 0:CAP], w2s[:, i, c, :], hT[:, i % 2, c, :],
                                    start=(c == 0), stop=(c == FC - 1))
                        ins.then_inc(eo_ps, 1)
                    else:
                        pe.wait_ge(eo_sb, n * E + min(E, experts_before(i)))
                        if i == 0:
                            pe.wait_ge(lg_r, n + 1)
                        if i >= 2:
                            pe.wait_ge(row_sb, n * NS + i - 1)
                        nc.tensor.transpose(bank[2 + i % 2][:, 0:P], eoT[:, i * P:(i + 1) * P], ident)\
                            .then_inc(row_ps, 1)

            gate_turned(0)
            omega()
            keep_warm(2)
            turn_logits(0)
            gate_turned(1)
            keep_warm(2)
            turn_logits(1)
            gate_last()
            pe.wait_ge(d_late, 16)
            pe.wait_ge(d_bw, 16)
            pe.wait_ge(d_cw, 16)
            M(bank[6][:, 0:2 * P], bw[:, :], basis_in, start=True, stop=True)
            M(bank[4][:, 0:P], basis_out, cwT[:, :], start=True, stop=True)
            M(bank[4][:, P:2 * P], basis_turned, cwT[:, :], start=True, stop=True).then_inc(set_ps, 1)
            pe.wait_ge(pool_set, 1)
            rank(0, 0)
            pe.wait_ge(tables, 1)
            nc.tensor.transpose(bank[4][:, 0:P], g1[:, 0:D], ident)
            nc.tensor.transpose(bank[4][:, P:2 * P], g2[:, 0:D], ident).then_inc(set_ps, 1)
            keep_warm(3, 5)
            pe.wait_ge(tables, 2)
            M(bank[4][:, 0:E], gT[:, 0:P], gate_c[:, 0:E], start=True, stop=True)
            M(bank[4][:, E:2 * E], gT[:, P:2 * P], gate_c[:, 0:E], start=True, stop=True).then_inc(set_ps, 1)
            keep_warm(10, 5)
            place(0, 0)
            pe.wait_ge(tables, 3)
            keep_warm(24)
            slots(0)

            def turn_u(b):
                pe.wait_ge(u_r, b + 1)
                if b >= 1:
                    pe.wait_ge(uT_sb, b)
                for c in range(TB):
                    ins = nc.tensor.transpose(bank[0][:, c * P:(c + 1) * P], u[:, b % 2, c, :], ident)
                ins.then_inc(uT_ps, 1)

            def read_out(b):
                pe.wait_ge(zc_r, b + 1)
                pe.wait_ge(zs_r, b + 1)
                if b >= 1:
                    pe.wait_ge(x2_r, b)
                for c in range(TB):
                    cs = slice(c * P, (c + 1) * P)
                    M(bank[6][:, cs], zc[:, b % 2, cs], g1[:, 0:D], start=True, stop=False)
                    ins = M(bank[6][:, cs], zs[:, b % 2, cs], g2[:, 0:D], start=False, stop=True)
                ins.then_inc(y_ps, 1)

            pe.wait_ge(row_sb, NS)
            keep_warm(27)
            pe.wait_ge(d_x1[0], 16)
            keep_warm(15)
            turn_u(0)
            keep_warm(2)

            def turn_w():
                pe.wait_ge(w_r, NB)
                pe.wait_ge(uT_sb, NB)
                for c in range(TB):
                    ins = nc.tensor.transpose(bank[0][:, c * P:(c + 1) * P], w[:, (NB - 1) % 2, c, :], ident)
                ins.then_inc(wT_ps, 1)

            def gate_w():
                pe.wait_ge(wT_sb, 1)
                pe.wait_ge(rank_read, piece(1, 0) + 1)
                for c in range(TB):
                    t = (NB - 1 - PIECES[1][-1][0]) * TB + c
                    ins = M(bank[2][:, t * E:(t + 1) * E], uT[:, NB % 2, c * P:(c + 1) * P], gate_c[:, 0:E],
                            start=True, stop=True)
                ins.then_inc(logits, 1)

            def read_out_last():
                pe.wait_ge(zc_r, NB)
                pe.wait_ge(zs_r, NB)
                pe.wait_ge(va_r, NB)
                pe.wait_ge(vq_sb, NB)
                for c in range(TB):
                    cs = slice(c * P, (c + 1) * P)
                    y = last_y(c)
                    M(y, zc[:, (NB - 1) % 2, cs], g1[:, :], start=True, stop=False)
                    ins = M(y, zs[:, (NB - 1) % 2, cs], g2[:, :], start=False, stop=True)
                ins.then_inc(y_ps, 1)

            for i in range(NB):
                pe.wait_ge(uT_sb, i + 1)
                if i >= 1:
                    pe.wait_ge(va_r, i)
                    pe.wait_ge(vq_sb, i)
                M(bank[4][:, :], bt[:, 0:P], uT[:, i % 2, :], start=True, stop=True)
                M(bank[5][:, :], bt[:, P:2 * P], uT[:, i % 2, :], start=True, stop=True).then_inc(v_ps, 1)
                if i == NB - 1:
                    gate_x2(i - 2)
                if i >= 1:
                    read_out(i - 1)
                if i + 1 < NB:
                    turn_u(i + 1)
                if i == 0:
                    keep_warm(6, 6)
                if i == ROUTE_FROM + 2:
                    rank(1, 0)
                if i == ROUTE_FROM + 4:
                    place(1, 0)
                if 0 <= i - 2 < NB - 3:
                    gate_x2(i - 2)
                if i == NB - 1:
                    turn_w()
                if i >= 1:
                    turn_x2(i - 1)
            rank(1, 1)
            gate_w()
            gate_x2(NB - 2)
            read_out_last()
            place(1, 1)
            rank(1, 2)
            keep_warm(8, 6)
            place(1, 2)
            keep_warm(16, 6)
            slots(1)


def shape_constants(np, P, E, SW, NSTRIP, NT):
    n = np.arange(P)
    eye = np.eye(P)
    k = np.arange(P) % (P // 2)
    rows = np.arange(1, P + 1)
    sines = -2.0 * np.sin(2 * np.pi * ((rows[:, None] * k[None, :]) % P) / P)
    sines[P // 2 - 1:, :] = 0.0
    low = (np.arange(NT)[None, :] % (NT // 2)) * P + n[:, None] + 1.0
    token_code = np.where(np.arange(NT)[None, :] < NT // 2, low, -low)
    early = np.concatenate([
        eye, sines,
        (n[:, None] <= n[None, :]).astype(float) - 1.0,
        np.tile(E - np.arange(E), (P, 1)), np.tile(np.arange(SW), (P, 1)), np.tile(np.arange(NSTRIP), (P, 1)),
        token_code], axis=1)
    q = np.arange(P // 2)
    cos = np.cos(2 * np.pi * ((n[:, None] * q[None, :]) % P) / P)
    sin = np.sin(2 * np.pi * ((n[:, None] * q[None, :]) % P) / P)
    alt = (-1.0) ** n
    re_in, im_in = cos, -sin
    im_in[:, 0] = alt
    re_out, im_out = 2.0 / P * cos, -2.0 / P * sin
    re_out[:, 0], im_out[:, 0] = 1.0 / P, alt / P
    late = np.concatenate([re_in, im_in, im_in, -re_in, re_out, im_out, im_out, -re_out], axis=1)
    return (eye - 1.0 / P).astype(np.float32), early.astype(np.float32), late.astype(np.float32)


def kernel(**inputs):
    import numpy as np
    import concourse.bacc as bacc
    from concourse.bass_utils import run_bass_kernel_spmd

    ins = {n: np.ascontiguousarray(inputs[n]) for n in (
        "L0_attn_u", "L0_attn_a_params", "L0_attn_B_w", "L0_attn_C_w", "L0_attn_D", "L0_ffn_gate_w", "L0_ffn_w1", "L0_ffn_w2")}
    x = ins["L0_attn_u"]
    shape, n_experts = x.shape, ins["L0_ffn_w1"].shape[0]
    center, early, late = shape_constants(np, 128, n_experts, 64, n_experts * 160 // 64, shape[0] * shape[1] // 128)
    arrays = {
        "x": x, "x_turned": np.ascontiguousarray(x.reshape(-1, shape[2]).T), "a_params": ins["L0_attn_a_params"],
        "b_w": ins["L0_attn_B_w"], "c_w_turned": np.ascontiguousarray(ins["L0_attn_C_w"].T), "d_skip": ins["L0_attn_D"],
        "gate_w": ins["L0_ffn_gate_w"], "w1": ins["L0_ffn_w1"], "w2": ins["L0_ffn_w2"],
        "const_center": center, "const_early": early, "const_late": late}
    nc = bacc.Bacc("TRN2", target_bir_lowering=False, num_devices=1)
    args = [nc.dram_tensor(n, a.shape, mybir.dt.from_np(a.dtype), kind="ExternalInput").ap()
            for n, a in arrays.items()]
    out = nc.dram_tensor("out", shape, mybir.dt.float32, kind="ExternalOutput").ap()
    macaron_moe_ssm_kernel(nc, *args, out)
    r = run_bass_kernel_spmd(nc, [arrays], core_ids=[0])
    return r.results[0]["out"]
```
